# Optimizing a Trainium2 kernel written in Bass

```python
import numpy as np
import jax
import jax.numpy as jnp

def _softmax(x, axis=-1):
    return jax.nn.softmax(x, axis=axis)

def _gelu(x):
    return jax.nn.gelu(x, approximate=True)

def _silu(x):
    return jax.nn.silu(x)

def _sigmoid(x):
    return jax.nn.sigmoid(x)

def _layernorm(x, axis=-1, eps=1e-05):
    m = jnp.mean(x, axis=axis, keepdims=True)
    v = jnp.var(x, axis=axis, keepdims=True)
    return (x - m) / jnp.sqrt(v + eps)

def _scatter_add(tgt, idx, src, axis=0):
    return tgt.at[idx].add(src)

def _segment_sum(src, seg, n):
    return jax.ops.segment_sum(src, seg, n)
kernel_name = 'mk_adj_preln_d4_adj_r2_65c21f'

def setup_inputs(seed: int=0):
    np.random.seed(seed)
    _w = jnp.asarray

    def _rec_inputs():
        import jax
        import jax.numpy as jnp
        _gk = jax.random.key(seed)
        x = -0.000929 + 1 * jax.random.normal(jax.random.fold_in(_gk, 1), (4096, 128), jnp.float32)
        _a = jax.random.bernoulli(jax.random.fold_in(_gk, 2), 0.00195312, (4096, 4096))
        _a = jnp.logical_or(_a, jnp.swapaxes(_a, -1, -2))
        _a = jnp.logical_or(_a, jnp.eye(4096, dtype=bool))
        adj = _a.astype(jnp.int32)
        return (x, adj)
    x, adj = _rec_inputs()

    def _L0_gnn_setup():
        import jax, jax.numpy as jnp
        import numpy as np
        NEG_BIG = -9000000000000000.0
        LEAKY_SLOPE = 0.2
        key = jax.random.key(seed)
        k1, k2, k3 = jax.random.split(key, 3)
        N, M, D = (4096, 4096, 128)
        qs = jax.random.normal(k1, (N, D), dtype=jnp.float32)
        ks = jax.random.normal(k2, (M, D), dtype=jnp.float32)
        HpGraph_e_k = jax.random.randint(k3, (N, M), 0, 2, dtype=jnp.int32)
        return {'qs': qs, 'ks': ks, 'HpGraph_e_k': HpGraph_e_k}
    _L0_gnn_all = _L0_gnn_setup()
    _L0_gnn_in = {k: v for k, v in _L0_gnn_all.items() if k in ('ks',)}
    del _L0_gnn_all

    def _L1_gnn_setup():
        import jax, jax.numpy as jnp
        import numpy as np
        N, IN_DIM, OUT_DIM, H = (2048, 128, 128, 4)
        HEAD_DIM = OUT_DIM // H
        NEG_SLOPE = 0.2
        key = jax.random.key(seed)
        k1, k2, k3, k4, k5 = jax.random.split(key, 5)
        x = jax.random.normal(k1, (N, IN_DIM), dtype=jnp.float32)
        adj = jax.random.randint(k2, (N, N), 0, 2, dtype=jnp.int32)
        W = jax.random.normal(k3, (OUT_DIM, IN_DIM), dtype=jnp.float32) * (1.0 / np.sqrt(IN_DIM))
        attn_src = jax.random.normal(k4, (1, H, HEAD_DIM), dtype=jnp.float32) * 0.1
        attn_dst = jax.random.normal(k5, (1, H, HEAD_DIM), dtype=jnp.float32) * 0.1
        return {'x': x, 'adj': adj, 'W': W, 'attn_src': attn_src, 'attn_dst': attn_dst}
    _L1_gnn_all = _L1_gnn_setup()
    _L1_gnn_in = {k: v for k, v in _L1_gnn_all.items() if k in ('W', 'attn_src', 'attn_dst')}
    del _L1_gnn_all

    def _L2_gnn_setup():
        import jax, jax.numpy as jnp
        import numpy as np
        ALPHA = 0.2
        NEG_INF = -9000000000000000.0
        key = jax.random.key(seed)
        k1, k2, k3, k4 = jax.random.split(key, 4)
        N, F_IN, F_OUT = (4096, 128, 128)
        h = jax.random.normal(k1, (N, F_IN), dtype=jnp.float32)
        adj = jax.random.randint(k2, (N, N), 0, 2, dtype=jnp.int32)
        W = jax.random.normal(k3, (F_IN, F_OUT), dtype=jnp.float32) * (1.414 / np.sqrt(F_IN))
        a = jax.random.normal(k4, (2 * F_OUT, 1), dtype=jnp.float32) * (1.414 / np.sqrt(2 * F_OUT))
        return {'h': h, 'adj': adj, 'W': W, 'a': a}
    _L2_gnn_all = _L2_gnn_setup()
    _L2_gnn_in = {k: v for k, v in _L2_gnn_all.items() if k in ('W', 'a')}
    del _L2_gnn_all

    def _L3_gnn_setup():
        import jax, jax.numpy as jnp
        import numpy as np
        NEG_INF = -9000000000000000.0
        ALPHA = 0.2
        key = jax.random.key(seed)
        k1, k2, k3, k4 = jax.random.split(key, 4)
        N, F_IN, H, D = (4096, 128, 4, 32)
        h = jax.random.normal(k1, (N, F_IN), dtype=jnp.float32)
        adj = jax.random.randint(k2, (N, N), 0, 2, dtype=jnp.int32)
        W = jax.random.normal(k3, (F_IN, H * D), dtype=jnp.float32) * (1.0 / np.sqrt(F_IN))
        a = jax.random.normal(k4, (1, H, 2 * D), dtype=jnp.float32)
        return {'h': h, 'adj': adj, 'W': W, 'a': a}
    _L3_gnn_all = _L3_gnn_setup()
    _L3_gnn_in = {k: v for k, v in _L3_gnn_all.items() if k in ('W', 'a')}
    del _L3_gnn_all
    return {'x': x, 'adj': adj, 'L0_gnn_ks': _L0_gnn_in['ks'], 'L1_gnn_W': _L1_gnn_in['W'], 'L1_gnn_attn_src': _L1_gnn_in['attn_src'], 'L1_gnn_attn_dst': _L1_gnn_in['attn_dst'], 'L2_gnn_W': _L2_gnn_in['W'], 'L2_gnn_a': _L2_gnn_in['a'], 'L3_gnn_W': _L3_gnn_in['W'], 'L3_gnn_a': _L3_gnn_in['a']}

def reference(x, adj, L0_gnn_ks, L1_gnn_W, L1_gnn_attn_src, L1_gnn_attn_dst, L2_gnn_W, L2_gnn_a, L3_gnn_W, L3_gnn_a):
    import jax
    import jax.numpy as jnp

    def _L0_gnn_ref(qs, ks, HpGraph_e_k):
        import jax, jax.numpy as jnp
        import numpy as np
        NEG_BIG = -9000000000000000.0
        LEAKY_SLOPE = 0.2
        scores = jnp.einsum('nd,md->nm', qs, ks)
        scores = jax.nn.leaky_relu(scores, negative_slope=LEAKY_SLOPE)
        scores = jnp.where(HpGraph_e_k > 0, scores, NEG_BIG)
        attn = jax.nn.softmax(scores, axis=1)
        return jnp.einsum('nm,md->nd', attn, ks)

    def _L1_gnn_ref(x, adj, W, attn_src, attn_dst):
        import jax, jax.numpy as jnp
        import numpy as np
        N, IN_DIM, OUT_DIM, H = (2048, 128, 128, 4)
        HEAD_DIM = OUT_DIM // H
        NEG_SLOPE = 0.2
        n = x.shape[0]
        h = (x @ W.T).reshape(n, H, HEAD_DIM)
        e_src = jnp.sum(h * attn_src, axis=-1)
        e_dst = jnp.sum(h * attn_dst, axis=-1)
        e = e_src[:, None, :] + e_dst[None, :, :]
        e = jax.nn.leaky_relu(e, negative_slope=NEG_SLOPE)
        e = jnp.where((adj == 0)[:, :, None], -jnp.inf, e)
        alpha = jax.nn.softmax(e, axis=1)
        out = jnp.einsum('ijh,jhd->ihd', alpha, h)
        return out.reshape(n, -1)

    def _L2_gnn_ref(h, adj, W, a):
        import jax, jax.numpy as jnp
        import numpy as np
        ALPHA = 0.2
        NEG_INF = -9000000000000000.0
        Wh = h @ W
        F_out = W.shape[1]
        e_src = Wh @ a[:F_out, 0]
        e_dst = Wh @ a[F_out:, 0]
        e = jax.nn.leaky_relu(e_src[:, None] + e_dst[None, :], negative_slope=ALPHA)
        attention = jax.nn.softmax(jnp.where(adj > 0, e, NEG_INF), axis=1)
        h_prime = attention @ Wh
        return h_prime

    def _L3_gnn_ref(h, adj, W, a):
        import jax, jax.numpy as jnp
        import numpy as np
        NEG_INF = -9000000000000000.0
        ALPHA = 0.2
        N = h.shape[0]
        H = a.shape[1]
        D = a.shape[2] // 2
        Wh = (h @ W).reshape(N, H, D)
        a_src = a[0, :, :D]
        a_dst = a[0, :, D:]
        s_src = jnp.einsum('nhd,hd->nh', Wh, a_src)
        s_dst = jnp.einsum('nhd,hd->nh', Wh, a_dst)
        e = s_src[:, None, :] + s_dst[None, :, :]
        e = jnp.where(e >= 0, e, ALPHA * e)
        e = jnp.where(adj[:, :, None] > 0, e, NEG_INF)
        attention = jax.nn.softmax(e, axis=1)
        h_prime = jnp.einsum('ijh,jhd->ihd', attention, Wh)
        return jax.nn.elu(h_prime.reshape(N, H * D))
    h = jnp.maximum(_layernorm(x, axis=-1), 0.0)
    x = x + _L0_gnn_ref(h, L0_gnn_ks, adj)
    h = jnp.maximum(_layernorm(x, axis=-1), 0.0)
    x = x + _L1_gnn_ref(h, adj, L1_gnn_W, L1_gnn_attn_src, L1_gnn_attn_dst)
    h = jnp.maximum(_layernorm(x, axis=-1), 0.0)
    x = x + _L2_gnn_ref(h, adj, L2_gnn_W, L2_gnn_a)
    h = jnp.maximum(_layernorm(x, axis=-1), 0.0)
    x = x + _L3_gnn_ref(h, adj, L3_gnn_W, L3_gnn_a)
    return x

_drawn_inputs = setup_inputs


def setup_inputs(seed=0):
    import zlib

    import numpy as np

    out = dict(_drawn_inputs(seed))
    spreads = {}
    factors = {'L1_gnn_attn_src': 6.687, 'L1_gnn_attn_dst': 2.682}
    for name, (base, spread) in spreads.items():
        noise = np.random.default_rng([zlib.crc32(name.encode()), seed]).standard_normal(out[name].shape)
        drawn = base * np.exp(spread * noise) if base else spread * noise
        out[name] = jnp.asarray(drawn.astype(out[name].dtype))
    for name, factor in factors.items():
        out[name] = (out[name] * factor).astype(out[name].dtype)
    return out
```

```python
from contextlib import ExitStack

import concourse.bass as bass
from concourse import mybir

F32 = mybir.dt.float32
BF16 = mybir.dt.bfloat16
I32 = mybir.dt.int32
U8 = mybir.dt.uint8
BYTES = {F32: 4, I32: 4, BF16: 2, U8: 1}
ALU = mybir.AluOpType
ACT = mybir.ActivationFunctionType
AX_X = mybir.AxisListType.X
RMAX = bass.bass_isa.ReduceOp.max

N, D, P = 4096, 128, 128
NT = N // P
CH = 512
NC = N // CH
Q = CH // P
EPS = 1e-5
SLOPE = 0.2
BIG = 2.0 ** 100
STEEP = 1e30
RING = 8
ON_ACT = (1, 3, 5, 7)
LAG = 2

HEADS = {1: 4, 2: 1, 3: 4}


def per(a, b):
    return a // b


def v_after(a, least):
    return not isinstance(a, int) or a >= least


def held(eng, a):
    return a if isinstance(a, int) else eng.snap(a)


def odd(a):
    return a % 2 if isinstance(a, int) else a & 1


class Shape:

    def __init__(self, heads):
        self.H = heads
        self.dh = D // heads
        self.w = self.dh + 1
        self.row = heads * 2 * 3 * self.w
        self.pairs = 2 if heads > 1 else 1
        self.split = heads == 1


def bass_gnn_stack_kernel(nc, x, adj, ks, w1, a1_src, a1_dst, w2, a2, w3, a3, out, layers=4):
    ctx = ExitStack()
    with ctx:
        top = [(nc.sbuf_base + 31) // 32 * 32]

        def place(name, shape, dtype, at=None):
            size = 1
            for n in shape[1:]:
                size *= n
            size *= BYTES[dtype]
            if at is None:
                at = top[0]
                top[0] = (at + size + 31) // 32 * 32
            return nc.alloc_sbuf_tensor_at(name, shape, dtype, offset=at)

        def place_bytes(name, shape, dtype):
            b = place(name, shape[:-1] + [shape[-1] * BYTES[dtype]], U8)
            return b, b[(slice(None),) * len(shape)].bitcast(dtype)

        def run(view, at, n, dtype):
            return view[(slice(None),) * (len(view.shape) - 1) + (bass.ds(at, n * BYTES[dtype]),)].bitcast(dtype)

        def sem(name):
            return ctx.enter_context(nc.semaphore(name))

        x_sb = place("x_sb", [P, NT, D], F32)
        ident = place("ident", [P, P], F32)
        identb = place("identb", [P, P], BF16)
        big_ident = place("big_ident", [P, P], BF16)
        ones_col = place("ones_col", [P, 1], F32)
        minus_half = place("minus_half", [P, NT], F32)
        minus_one = place("minus_one", [P, Q], F32)
        w_ext = {L: place(f"w_ext{L}", [P, D + 2 * HEADS[L]], F32) for L in HEADS}
        stats = place("stats", [P, NT, 6], F32)
        mean = place("mean", [P, NT], F32)
        rstd = place("rstd", [P, NT], F32)
        st_tmp = place("st_tmp", [P, 5, NT], F32)
        phase = top[0]

        ks_T = place("ks_T", [P, N], F32)
        ks_nat = place("ks_nat", [P, NT, D], F32)
        adj_in = place("adj_in", [P, 2, N], I32)
        mask = place("mask", [P, 2, N], BF16)
        relu4 = place("relu4", [P, 4, CH], F32)
        score = place("score", [P, 2, N], F32)
        prob_T = place("prob_T", [P, 4, CH], F32)
        adjT_out = place("adjT_out", [P, 2, NT, P], BF16)
        h_T = place("h_T", [P, N], F32)
        h_tile = place("h_tile", [P, 2, P], F32)
        norm0 = place("norm0", [P, 2, Q, D], F32)
        row_max = place("row_max", [P, 2, NC], F32)
        row_top = place("row_top", [P, 2], F32)
        neg_max = place("neg_max", [P, 2], F32)
        row_sum = place("row_sum", [P, 2, NC], F32)
        den0 = place("den0", [P, 2], F32)
        rden0 = place("rden0", [P, 2], F32)
        w_in = place("w_in", [P, 3, P], F32)
        w_turn = place("w_turn", [P, 3, P], F32)
        a_blk = place("a_blk", [P, 3, 8], F32)

        top[0] = phase
        TROW = max(Shape(h).row for h in HEADS.values())
        WMAX = max(Shape(h).w for h in HEADS.values())
        table_b, table = place_bytes("table", [P, NT * TROW], BF16)
        adjT_b, adjT = place_bytes("adjT", [P, Q, 2 * NT * P], BF16)
        s_bc_b, s_bc = place_bytes("s_bc", [P, 4 * CH], F32)
        at = top[0]
        norm = place("norm", [P, 2, Q, D], F32)
        h_grp = place("h_grp", [P, 2, CH], F32)
        steps = place("steps", [P, RING, CH], BF16, at=at)
        gates = place("gates", [P, len(ON_ACT), CH], BF16)
        at = top[0]
        prod = place("prod", [P, 2, 1056], F32)
        rest = place("rest", [P, 2, 1056], F32)
        after = top[0]
        top[0] = at
        red = place("red", [P, 2, 2 * Q * WMAX], F32)
        red_a = place("red_a", [P, 2, Q * 33], F32)
        pt = [place(f"pt{i}", [P, Q * WMAX], F32) for i in range(3)]
        assert top[0] <= after
        top[0] = after
        at = top[0]
        wh = place("wh", [P, NT, D], F32)
        o_all = place("o_all", [P, NT, D], F32, at=at)
        s_row = place("s_row", [4, 2, CH], F32)
        sd = place("sd", [P, NT, 8], F32)
        d_max = place("d_max", [P, 4], F32)
        d_top = place("d_top", [P, 4], F32)
        d_rel = place("d_rel", [P, NT * 4], F32)
        s_lim = place("s_lim", [P, 2, NT * 4], F32)
        s_top = place("s_top", [P, NT * 4], F32)
        ef = place("ef", [P, 2, NT * 4], F32)
        ab = place("ab", [P, 2, NT * 4], F32)
        neg_d_b, neg_d = place_bytes("neg_d", [P, NT * 4], F32)
        steep_b, steep_d = place_bytes("steep_d", [P, 2, NT * 4], F32)
        waited = place("waited", [P, 1], F32)
        rden = place("rden", [P, Q], F32)
        assert top[0] <= nc.sbuf_usable_end, top[0]

        ps = ctx.enter_context(nc.psum_tensor("ps", [P, 8 * CH], F32))
        ps_b = ps[:, :].bitcast(BF16)

        adjT_d = nc.dram_tensor("adjT_d", [NT, P, NT * P], BF16).ap()
        s_d = {L: nc.dram_tensor(f"s_d{L}", [HEADS[L], N], F32).ap() for L in HEADS}

        loaded = {n: sem(f"loaded_{n}") for n in ("x", "ks", "w", "a")}
        set_up = sem("set_up")
        w_turned = sem("w_turned")
        w_copied = sem("w_copied")
        wa_ready = sem("wa_ready")
        w_done = sem("w_done")
        ks_turned = sem("ks_turned")
        ks_copied = sem("ks_copied")
        adj_loaded = [sem("adj_loaded0"), sem("adj_loaded1")]
        mask_ready = sem("mask_ready")
        h_tile_ready = sem("h_tile_ready")
        s_ready = sem("s_ready")
        relu_ready = sem("relu_ready")
        score_ready = sem("score_ready")
        neg_ready = sem("neg_ready")
        p_ready = sem("p_ready")
        turned = sem("turned")
        prob_ready = sem("prob_ready")
        prob_used = sem("prob_used")
        mt_turned = sem("mt_turned")
        mt_copied = sem("mt_copied")
        adjT_stored = [sem("adjT_stored0"), sem("adjT_stored1")]
        x_ready = {L: sem(f"x_ready{L}") for L in range(4)}
        row_step = sem("row_step")
        stored = sem("stored")

        block = ctx.enter_context(nc.Block())

        ig_of = lambda L, m: per(m, Shape(HEADS[L]).pairs)
        S = {}
        for L in [0] + list(HEADS):
            names = ["stat", "stat_step", "var", "rstd", "normed", "h_turned", "h_done"]
            if L:
                names += ["proj", "proj_wh", "proj_sd", "s_row_turned", "s_row_copied", "d_max", "d_top", "s_top",
                          "rel", "ef", "neg", "prod", "prod1", "ones", "hi", "r1", "mid", "table", "s_stored0", "s_stored1",
                          "adjT_in", "s_bc_in", "gate", "gate_used", "step", "step_used", "reduced", "pool_step"]
            S[L] = {n: sem(f"L{L}_{n}") for n in names}
        tail = {n: sem(f"tail_{n}") for n in ("neg", "exp", "sum", "y")}
        X_DONE = {0: NT, 1: 32, 2: 8, 3: 32}

        def layer0_stored(eng):
            for done in adjT_stored:
                eng.wait_ge(done, 16 * NT // 2)

        def layer_dma(sp, L):
            s, c = S[L], Shape(HEADS[L])

            def load_adjT(ig, parity):
                sp.dma_start(adjT[:, :, parity * NT * P:(parity + 1) * NT * P],
                             adjT_d[bass.ds(ig * Q, Q)].rearrange("q p c -> p q c")).then_inc(s["adjT_in"], 16)

            def load_s(m):
                ig = ig_of(L, m)
                if c.split:
                    rows, slot, n = 0, odd(m), 1
                else:
                    rows, slot, n = odd(m) * 2, odd(m) * 2, 2
                src = s_d[L][bass.ds(rows, n), bass.ds(ig * CH, CH)]
                sp.dma_start(s_bc[:, bass.ds(slot * CH, n * CH)].rearrange("p (h c) -> p h c", h=n), src.partition_broadcast(P)).then_inc(s["s_bc_in"], 16)

            sp.wait_ge(x_ready[L - 1], X_DONE[L - 1])
            load_adjT(0, 0)
            with sp.Fori(0, NC // 2, 1) as g_at:
                g = g_at * 2
                for parity in range(2):
                    sp.wait_ge(s["s_row_copied"], g + parity + 1)
                    sp.dma_start(s_d[L][:, bass.ds((g + parity) * CH, CH)],
                                 s_row[0:c.H, parity, :]).then_inc(s[f"s_stored{parity}"], 16)
            for parity in range(2):
                sp.wait_ge(s[f"s_stored{parity}"], 16 * NC // 2)
            load_s(0)
            sp.wait_ge(s["s_bc_in"], 16)
            load_s(1)
            sp.wait_ge(s["table"], NC)
            sp.wait_ge(s["adjT_in"], 16)
            load_adjT(1, 1)

            def next_s(m):
                sp.wait_ge(s["gate_used"], 2 * (m + 1) * (NT // RING) * len(ON_ACT))
                sp.wait_ge(s["s_bc_in"], 16 * (m + 2))
                load_s(m + 2)

            with sp.Fori(0, NC // 2 - 1, 1) as ig_at:
                for parity in range(2):
                    ig = ig_at * 2 + parity
                    for pp in range(c.pairs):
                        next_s(ig * c.pairs + pp)
                    sp.wait_ge(s["step_used"], (ig + 1) * 2 * c.pairs * NT)
                    sp.wait_ge(s["adjT_in"], 16 * (ig + 2))
                    load_adjT(ig + 2, parity)
            for m in range((NC - 2) * c.pairs, NC * c.pairs - 2):
                next_s(m)

        @block.sync
        def _(sp):
            sp.dma_start(x_sb[:, :, :], x.rearrange("(t p) d -> p t d", p=P)).then_inc(loaded["x"], 16)
            sp.dma_start(ks_nat[:, :, :], ks.rearrange("(t p) d -> p t d", p=P)).then_inc(loaded["ks"], 16)

            def load_adj(t, parity):
                sp.dma_start(adj_in[:, parity, :], adj_tiles(t)).then_inc(adj_loaded[parity], 16)

            def adj_tiles(t):
                return adj[bass.ds(t * P, P), :]

            load_adj(0, 0)
            for i, w in enumerate((w1, w2, w3)):
                sp.dma_start(w_in[:, i, :], w).then_inc(loaded["w"], 16)
            sp.wait_ge(set_up, 5)
            n = 0
            for h in range(4):
                rows = slice(32 * h, 32 * h + 32)
                for src, i, col in ((a1_src[0, h], 0, h), (a1_dst[0, h], 0, 4 + h),
                                    (a3[0, h, 0:32], 2, h), (a3[0, h, 32:64], 2, 4 + h)):
                    sp.dma_start(a_blk[rows, i, col:col + 1], src.unsqueeze(1)).then_inc(loaded["a"], 16)
                    n += 1
            for k in range(2):
                sp.dma_start(a_blk[:, 1, k:k + 1], a2[k * D:(k + 1) * D, :]).then_inc(loaded["a"], 16)
                n += 1
            assert n == 18
            load_adj(1, 1)

            def step(t, parity, more=True):
                if more:
                    sp.wait_ge(mask_ready, (t + 1) * NC)
                    load_adj(t + 2, parity)
                sp.wait_ge(mt_copied, (t + 1) * NC)
                sp.dma_start(adjT_d[bass.ds(t, 1)].rearrange("a p c -> (a p) c"),
                             adjT_out[:, parity].rearrange("p t c -> p (t c)")).then_inc(adjT_stored[parity], 16)

            with sp.Fori(0, NT // 2 - 1, 1) as t_at:
                t = t_at * 2
                step(t, 0)
                step(t + 1, 1)
            step(NT - 2, 0, more=False)
            step(NT - 1, 1, more=False)
            layer0_stored(sp)

            for L in HEADS:
                if L >= layers:
                    break
                layer_dma(sp, L)
            if layers < 4:
                sp.wait_ge(x_ready[layers - 1], X_DONE[layers - 1])
                sp.dma_start(out.rearrange("(t p) d -> p t d", p=P), x_sb[:, :, :]).then_inc(stored, 16)
                sp.wait_ge(stored, 16)
            else:
                with sp.Fori(0, NC, 1) as g:
                    sp.wait_ge(tail["y"], g + 1)
                    sp.dma_start(out[bass.ds(g * CH, CH), :].rearrange("(t p) d -> p t d", p=P),
                                 x_sb[:, bass.ds(g * Q, Q), :]).then_inc(stored, 16)
                sp.wait_ge(stored, 16 * NC)

        def rstd_pow(pool, L):
            s = S[L]
            pool.wait_ge(s["var"], 1)
            nc.gpsimd.tensor_tensor(rstd[:, :], st_tmp[:, 4, :], minus_half[:, :], ALU.pow).then_inc(s["rstd"], 1)

        def layer_pool(pool, L):
            s, c = S[L], Shape(HEADS[L])
            H, dh, w = c.H, c.dh, c.w
            pool.wait_ge(s["d_max"], 1)
            nc.gpsimd.partition_all_reduce(d_top[:, 0:H], d_max[:, 0:H], P, RMAX).then_inc(s["d_top"], 1)

            def table_part(g, parity):
                pv = prod[:, parity, 0:Q * H * 2 * w].rearrange("p (t h e w) -> p t h e w", t=Q, h=H, e=2)
                efv = ef[:, :, 0:NT * H].rearrange("p e (t h) -> p e t h", h=H)
                pool.wait_ge(s["ef"], 2)
                if not isinstance(g, int) or g >= 2:
                    pool.wait_ge(s["r1"], g - 1)
                for e in range(2):
                    last = nc.gpsimd.tensor_copy(pv[:, :, :, e, dh], efv[:, e, bass.ds(g * Q, Q), :]
                                                 ).then_inc(s["ones"], 1)
                pool.wait_ge(s["ones"], 2 * (g + 1))
                nc.gpsimd.tensor_tensor(
                    pv[:, :, :, 1, 0:dh],
                    wh[:, bass.ds(g * Q, Q), :].rearrange("p t (h d) -> p t h d", h=H),
                    efv[:, 1, bass.ds(g * Q, Q), :].unsqueeze(3).to_broadcast([P, Q, H, dh]),
                    ALU.mult).then_inc(s["prod1"], 1)

            table_part(0, 0)
            table_part(1, 1)
            with pool.Fori(1, NC // 2, 1) as g_at:
                g = g_at * 2
                table_part(g, 0)
                table_part(g + 1, 1)

            view = lambda a: a[:, 0:Q * w].rearrange("p (q w) -> p q w", q=Q)
            ta, tb, tc = (view(a) for a in pt)

            def combine(n, ig, h, e_sum, f_sum, a_sum):
                base = n * KSTEP
                k = [0]

                def wait():
                    pool.wait_ge(s["pool_step"], base + k[0])

                def done(ins):
                    k[0] += 1
                    ins.then_inc(s["pool_step"], 1)

                abv = ab[:, :, 0:NT * H].rearrange("p e (t h) -> p e t h", h=H)

                def factor(e, width):
                    return abv[:, e, bass.ds(ig * Q, Q), bass.ds(h, 1)].to_broadcast([P, Q, width])

                if not c.split:
                    done(nc.gpsimd.tensor_tensor(tb, a_sum, f_sum, ALU.subtract))
                    wait()
                    f_sum = tb
                done(nc.gpsimd.tensor_tensor(tc, f_sum, factor(1, w), ALU.mult))
                done(nc.gpsimd.tensor_tensor(ta, e_sum, factor(0, w), ALU.mult))
                wait()
                done(nc.gpsimd.tensor_tensor(tb, ta, tc, ALU.add))
                wait()
                done(nc.gpsimd.tensor_tensor(rden[:, :], tb[:, :, dh], minus_one[:, :], ALU.pow))
                wait()
                rb = rden[:, :].unsqueeze(2).to_broadcast([P, Q, dh])
                cols = bass.ds(h * dh, dh)
                if L == 3:
                    nc.gpsimd.tensor_tensor(o_all[:, bass.ds(ig * Q, Q), cols], tb[:, :, 0:dh], rb, ALU.mult
                                            ).then_inc(x_ready[L], 1)
                else:
                    done(nc.gpsimd.tensor_tensor(ta[:, :, 0:dh], tb[:, :, 0:dh], rb, ALU.mult))
                    wait()
                    xv = x_sb[:, bass.ds(ig * Q, Q), cols]
                    nc.gpsimd.tensor_tensor(xv, xv, ta[:, :, 0:dh], ALU.add).then_inc(x_ready[L], 1)
                pool.wait_ge(x_ready[L], n + 1)
                assert k[0] == KSTEP

            KSTEP = (4 if c.split else 5) + (L != 3)

            with pool.Fori(0, NC * c.pairs, 1) as m:
                ig = ig_of(L, m)
                if c.split:
                    pool.wait_ge(s["reduced"], 2 * (m + 1))
                    combine(m, ig, 0, view(red[:, 0]), view(red[:, 1]), None)
                else:
                    for hf in range(2):
                        n = m * 2 + hf
                        pool.wait_ge(s["reduced"], n + 1)
                        rv = red[:, hf, 0:Q * 2 * w].rearrange("p (q e w) -> p q e w", q=Q, e=2)
                        combine(n, ig, odd(m) * 2 + hf, rv[:, :, 0, :], rv[:, :, 1, :], view(red_a[:, hf]))

        @block.gpsimd
        def _(pool):
            nc.gpsimd.memset(ident[:, :], 0.0).then_inc(set_up, 1)
            nc.gpsimd.memset(ones_col[:, :], 1.0).then_inc(set_up, 1)
            nc.gpsimd.memset(minus_half[:, :], -0.5).then_inc(set_up, 1)
            nc.gpsimd.memset(a_blk[:, :, :], 0.0).then_inc(set_up, 1)
            nc.gpsimd.memset(minus_one[:, :], -1.0).then_inc(set_up, 1)
            pool.wait_ge(set_up, 5)
            nc.gpsimd.affine_select(out=ident[:, :], in_=ident[:, :], compare_op=ALU.not_equal, fill=1.0,
                                    base=0, pattern=[[-1, P]], channel_multiplier=1).then_inc(set_up, 1)
            pool.wait_ge(set_up, 6)
            nc.gpsimd.tensor_copy(identb[:, :], ident[:, :]).then_inc(set_up, 1)
            nc.gpsimd.tensor_scalar(big_ident[:, :], ident[:, :], BIG, 0.0, ALU.mult, ALU.add).then_inc(set_up, 1)

            rstd_pow(pool, 0)

            def step(t, parity):
                pool.wait_ge(s_ready, t * NC)
                nc.gpsimd.tensor_copy(h_tile[:, 1 - parity, :], h_T[:, bass.ds((t + 1) * P, P)]
                                      ).then_inc(h_tile_ready, 1)

            pool.wait_ge(S[0]["h_done"], NC)
            nc.gpsimd.tensor_copy(h_tile[:, 0, :], h_T[:, 0:P]).then_inc(h_tile_ready, 1)
            step(0, 0)
            with pool.Fori(0, NT // 2 - 1, 1) as t_at:
                t = t_at * 2 + 1
                step(t, 1)
                step(t + 1, 0)

            for L in HEADS:
                if L >= layers:
                    break
                rstd_pow(pool, L)
                layer_pool(pool, L)

        def h_relu(act, L):
            s = S[L]
            if L == 1:
                layer0_stored(act)

            def group(g, parity):
                act.wait_ge(s["h_turned"], g + 1)
                if L == 0:
                    dst = h_T[:, bass.ds(g * CH, CH)]
                else:
                    dst = h_grp[:, parity, :]
                    if not isinstance(g, int) or g >= 2:
                        act.wait_ge(s["proj"], g - 1)
                nc.scalar.activation(dst, ps[:, parity * CH:(parity + 1) * CH], ACT.Relu).then_inc(s["h_done"], 1)
                if L:
                    act.wait_ge(s["proj"], g + 1)
                    src = ps[:, (2 + 2 * parity) * CH:(4 + 2 * parity) * CH].rearrange("p (q c) -> p q c", q=Q)
                    nc.scalar.copy(wh[:, bass.ds(g * Q, Q), :], src[:, :, 0:D]).then_inc(s["proj_wh"], 1)

            group(0, 0)
            group(1, 1)
            with act.Fori(1, NC // 2, 1) as g_at:
                g = g_at * 2
                group(g, 0)
                group(g + 1, 1)

        def layer_act(act, L):
            s, c = S[L], Shape(HEADS[L])
            H, w = c.H, c.w
            n = NT * H
            h_relu(act, L)
            act.wait_ge(s["rel"], 1)
            nc.scalar.activation(ef[:, 0, 0:n], d_rel[:, 0:n], ACT.Exp).then_inc(s["ef"], 1)
            nc.scalar.activation(ef[:, 1, 0:n], d_rel[:, 0:n], ACT.Exp, scale=SLOPE).then_inc(s["ef"], 1)
            act.wait_ge(s["rel"], 3)
            nc.scalar.activation(ab[:, :, 0:n], s_lim[:, :, 0:n], ACT.Exp).then_inc(s["ef"], 1)

            def table_part(g, parity):
                act.wait_ge(s["prod"], g + 1)
                act.wait_ge(s["prod1"], g + 1)
                nc.scalar.copy(table_view(g, 0, c), prod_view(prod, parity, c)).then_inc(s["hi"], 1)
                act.wait_ge(s["r1"], g + 1)
                nc.scalar.copy(table_view(g, 1, c), prod_view(rest, parity, c)).then_inc(s["mid"], 1)

            with act.Fori(0, NC // 2, 1) as g_at:
                g = g_at * 2
                table_part(g, 0)
                table_part(g + 1, 1)

            act.wait_ge(s["neg"], 3 if c.split else 2)
            A = len(ON_ACT)

            def units(row, col, gi, hf, first):
                for i, k in enumerate(ON_ACT):
                    if not first:
                        act.wait_ge(s["gate_used"], gi + i + 1 - A)
                    sign = -1.0 if c.split and hf else 1.0
                    bias = run(steep_b[:, hf if c.split else 0], col + k * H * 4, 1, F32)
                    nc.scalar.activation(gates[:, i, :], row, ACT.Sigmoid, bias=bias,
                                         scale=sign * STEEP).then_inc(s["gate"], 1)

            def pair(m):
                act.wait_ge(s["s_bc_in"], 16 * (m + 1))
                for hf in range(2):
                    row = s_slot(act, c, m, hf)
                    d0 = 0 if c.split else held(act, odd(m) * 8 + hf * 4)
                    g0 = held(act, (m * 2 + hf) * (NT // RING * A))
                    start = isinstance(m, int) and m == 0 and hf == 0
                    if c.split and not start:
                        act.wait_ge(s["gate_used"], g0)
                        nc.scalar.copy(waited[:, :], ones_col[:, :])
                        start = True
                    units(row, d0, g0, hf, start)
                    with act.Fori(1, NT // RING, 1) as j_at:
                        units(row, held(act, j_at * (RING * H * 4) + d0), held(act, g0 + j_at * A), hf, False)

            pair(0)
            with act.Fori(1, NC * c.pairs, 1) as m:
                pair(m)

        def s_slot(eng, c, m, hf):
            slot = held(eng, odd(m) * (CH * 4) if c.split else odd(m) * (2 * CH * 4) + hf * CH * 4)
            return run(s_bc_b, slot, CH, F32)

        def table_view(g, part, c):
            t = table[:, :].rearrange("p (t r) -> p t r", t=NT)[:, bass.ds(g * Q, Q), 0:c.row]
            return t.rearrange("p t (b s w) -> p t b s w", s=3, w=c.w)[:, :, :, part, :]

        def prod_view(b, parity, c):
            return b[:, parity, 0:Q * c.H * 2 * c.w].rearrange("p (t b w) -> p t b w", t=Q, w=c.w)

        @block.scalar
        def _(act):
            for g in range(NC):
                act.wait_ge(ks_turned, g + 1)
                nc.scalar.copy(ks_T[:, g * CH:(g + 1) * CH], ps[:, (g % 2) * CH:(g % 2 + 1) * CH]).then_inc(ks_copied, 1)
            h_relu(act, 0)
            act.wait_ge(set_up, 8)

            def step(t, parity, scores=True, probs=True):
                v, vp = t - 1, 1 - parity
                first = isinstance(t, int)
                for ch in range(NC):
                    if probs:
                        nv = v * NC + ch
                        if ch == 0:
                            act.wait_ge(neg_ready, v + 1)
                            if v_after(v, 1):
                                act.wait_ge(row_step, 3 * v - 2)
                        sl = score[:, vp, ch * CH:(ch + 1) * CH]
                        nc.scalar.activation(sl, sl, ACT.Exp, bias=neg_max[:, vp:vp + 1],
                                             accum_out=row_sum[:, vp, ch:ch + 1]).then_inc(p_ready, 1)
                    if scores:
                        n = t * NC + ch
                        act.wait_ge(s_ready, n + 1)
                        if not first or n >= 4:
                            act.wait_ge(score_ready, n - 3)
                        nc.scalar.activation(relu4[:, ch % 4, :], ps[:, (ch % 4) * CH:(ch % 4 + 1) * CH], ACT.Relu,
                                             scale=1.0 / SLOPE - 1.0).then_inc(relu_ready, 1)
                        act.wait_ge(mt_turned, n + 1)
                        if ch == 0 and (not first or t >= 2):
                            act.wait_ge(adjT_stored[parity], 16 * per(t, 2))
                        mt = ps_b[:, 4 * 2 * CH:4 * 2 * CH + CH]
                        nc.scalar.activation(adjT_out[:, parity, ch * Q:(ch + 1) * Q, :].rearrange("p t c -> p (t c)"),
                                             mt, ACT.Identity, bias=ones_col[:, 0:1]).then_inc(mt_copied, 1)

            step(0, 0, probs=False)
            step(1, 1)
            with act.Fori(1, NT // 2, 1) as t_at:
                t = t_at * 2
                step(t, 0)
                step(t + 1, 1)
            step(NT, 0, scores=False)

            for L in HEADS:
                if L >= layers:
                    break
                layer_act(act, L)
            if layers == 4:
                with act.Fori(0, NC // 2, 1) as g_at:
                    g = g_at * 2
                    for parity in range(2):
                        act.wait_ge(tail["neg"], g + parity + 1)
                        v = s_bc[:, parity * CH:(parity + 1) * CH]
                        nc.scalar.activation(v, v, ACT.Exp).then_inc(tail["exp"], 1)

        def layer_stats(dve, L):
            s = S[L]
            if L == 0:
                dve.wait_ge(loaded["x"], 16)
            else:
                dve.wait_ge(x_ready[L - 1], X_DONE[L - 1])
            if L == 1:
                layer0_stored(dve)
            with dve.Fori(0, NT // 4, 1) as t_at:
                t = t_at * 4
                for k in range(4):
                    nc.vector.bn_stats(stats[:, bass.ds(t + k, 1), :].rearrange("p a b -> p (a b)"),
                                       x_sb[:, bass.ds(t + k, 1), :].rearrange("p a b -> p (a b)")).then_inc(s["stat"], 1)
            dve.wait_ge(s["stat"], NT)
            k = [0]

            def link(ins):
                k[0] += 1
                ins.then_inc(s["stat_step"], 1)
                dve.wait_ge(s["stat_step"], k[0])

            me, mo, ve, vo = (stats[:, :, i] for i in (1, 4, 2, 5))
            t0, t1, t2, t3, veps = (st_tmp[:, i, :] for i in range(5))
            link(nc.vector.tensor_tensor(t0, me, mo, ALU.add))
            link(nc.vector.tensor_tensor(t1, me, mo, ALU.subtract))
            link(nc.vector.tensor_tensor(t2, ve, vo, ALU.add))
            link(nc.vector.scalar_tensor_tensor(out=t3, in0=t1, scalar=0.25, in1=t1, op0=ALU.mult, op1=ALU.mult))
            link(nc.vector.tensor_scalar(mean[:, :], t0, 0.5, None, ALU.mult))
            link(nc.vector.tensor_scalar(t2, t2, 1.0 / D, EPS, ALU.mult, ALU.add))
            nc.vector.tensor_tensor(veps, t2, t3, ALU.add).then_inc(s["var"], 1)

        def layer_norm(dve, L):
            s = S[L]
            buf = norm0 if L == 0 else norm
            dve.wait_ge(s["rstd"], 1)

            def group(g, parity):
                if not isinstance(g, int) or g >= 2:
                    dve.wait_ge(s["h_turned"], g - 1)
                for q in range(Q):
                    t = g * Q + q
                    nc.vector.tensor_scalar(buf[:, parity, q, :], x_sb[:, bass.ds(t, 1), :].rearrange("p a b -> p (a b)"),
                                            mean[:, bass.ds(t, 1)], rstd[:, bass.ds(t, 1)],
                                            ALU.subtract, ALU.mult).then_inc(s["normed"], 1)
                if L and (not isinstance(g, int) or g >= 1):
                    after_projection(g - 1, 1 - parity)

            def after_projection(g, parity):
                c = Shape(HEADS[L])
                dve.wait_ge(s["proj_wh"], g + 1)
                src = ps[:, (2 + 2 * parity) * CH:(4 + 2 * parity) * CH].rearrange("p (q c) -> p q c", q=Q)
                nc.vector.tensor_copy(sd[:, bass.ds(g * Q, Q), 0:2 * c.H], src[:, :, D:D + 2 * c.H]).then_inc(s["proj_sd"], 1)
                dve.wait_ge(s["s_row_turned"], g + 1)
                if not isinstance(g, int) or g >= 2:
                    dve.wait_ge(s[f"s_stored{parity}"], 16 * per(g, 2))
                nc.vector.tensor_copy(s_row[0:c.H, parity, :], ps[0:c.H, (6 + parity) * CH:(7 + parity) * CH]
                                      ).then_inc(s["s_row_copied"], 1)

            group(0, 0)
            group(1, 1)
            with dve.Fori(1, NC // 2, 1) as g_at:
                g = g_at * 2
                group(g, 0)
                group(g + 1, 1)
            if L:
                after_projection(NC - 1, 1)

        def layer_dve(dve, L):
            s, c = S[L], Shape(HEADS[L])
            H, dh, w = c.H, c.dh, c.w
            n = NT * H
            dve.wait_ge(s["proj_sd"], NC)
            nc.vector.tensor_reduce(d_max[:, 0:H], sd[:, :, H:2 * H].rearrange("p t h -> p h t"), AX_X, ALU.max
                                    ).then_inc(s["d_max"], 1)
            flat = lambda a: a.rearrange("p (t h) -> p t h", h=H)
            sv, dv = sd[:, :, 0:H], sd[:, :, H:2 * H]
            nc.vector.tensor_scalar(flat(neg_d[:, 0:n]), dv, -1.0, None, ALU.mult).then_inc(s["neg"], 1)
            nc.vector.tensor_scalar(flat(steep_d[:, 0, 0:n]), dv, STEEP, None, ALU.mult).then_inc(s["neg"], 1)
            if c.split:
                nc.vector.tensor_scalar(flat(steep_d[:, 1, 0:n]), dv, -STEEP, None, ALU.mult).then_inc(s["neg"], 1)
            dve.wait_ge(s["d_top"], 1)
            tb = d_top[:, 0:H].unsqueeze(1).to_broadcast([P, NT, H])
            nc.vector.tensor_tensor(flat(d_rel[:, 0:n]), dv, tb, ALU.subtract).then_inc(s["rel"], 1)
            nc.vector.tensor_tensor(flat(s_top[:, 0:n]), sv, tb, ALU.add).then_inc(s["s_top"], 1)
            dve.wait_ge(s["s_top"], 1)
            nc.vector.tensor_scalar(s_lim[:, 0, 0:n], s_top[:, 0:n], 1.0 - SLOPE, 0.0, ALU.mult, ALU.min).then_inc(s["rel"], 1)
            nc.vector.tensor_scalar(s_lim[:, 1, 0:n], s_top[:, 0:n], SLOPE - 1.0, 0.0, ALU.mult, ALU.min).then_inc(s["rel"], 1)

            def product(g, parity):
                pv = prod[:, parity, 0:Q * H * 2 * w].rearrange("p (t h e w) -> p t h e w", t=Q, h=H, e=2)
                efv = ef[:, :, 0:n].rearrange("p e (t h) -> p e t h", h=H)
                if not isinstance(g, int) or g >= 2:
                    dve.wait_ge(s["hi"], g - 1)
                    dve.wait_ge(s["r1"], g - 1)
                nc.vector.tensor_tensor(
                    pv[:, :, :, 0, 0:dh], wh[:, bass.ds(g * Q, Q), :].rearrange("p t (h d) -> p t h d", h=H),
                    efv[:, 0, bass.ds(g * Q, Q), :].unsqueeze(3).to_broadcast([P, Q, H, dh]), ALU.mult).then_inc(s["prod"], 1)

            def parts(g, parity):
                pv, rv = prod_view(prod, parity, c), prod_view(rest, parity, c)
                dve.wait_ge(s["hi"], g + 1)
                if not isinstance(g, int) or g >= 2:
                    dve.wait_ge(s["mid"], g - 1)
                    dve.wait_ge(s["table"], g - 1)
                nc.vector.tensor_tensor(rv, pv, table_view(g, 0, c), ALU.subtract).then_inc(s["r1"], 1)
                dve.wait_ge(s["mid"], g + 1)
                dve.wait_ge(s["r1"], g + 1)
                nc.vector.tensor_tensor(table_view(g, 2, c), rv, table_view(g, 1, c), ALU.subtract).then_inc(s["table"], 1)

            dve.wait_ge(s["ef"], 1)
            dve.wait_ge(s["proj_wh"], NC)
            product(0, 0)
            product(1, 1)
            parts(0, 0)
            parts(1, 1)
            with dve.Fori(1, NC // 2, 1) as g_at:
                g = g_at * 2
                product(g, 0)
                product(g + 1, 1)
                parts(g, 0)
                parts(g + 1, 1)

            A = len(ON_ACT)
            dve.wait_ge(s["neg"], 3 if c.split else 2)

            def units(row, col, gi, u, mk, hf, first):
                for k in range(RING):
                    if k % 2 == 0 and not first:
                        dve.wait_ge(s["step_used"], u + (k + 2 - RING))
                    dst = steps[:, k, :].rearrange("p (q c) -> p q c", q=Q)
                    if k in ON_ACT:
                        i = ON_ACT.index(k)
                        dve.wait_ge(s["gate"], gi + i + 1)
                        nc.vector.tensor_tensor(dst, gates[:, i, :].rearrange("p (q c) -> p q c", q=Q), mk(k), ALU.mult
                                                ).then_inc(s["gate_used"], 1)
                        continue
                    op = ALU.is_lt if c.split and hf else ALU.is_ge
                    nc.vector.scalar_tensor_tensor(out=dst, in0=row, scalar=run(neg_d_b, col + k * H * 4, 1, F32),
                                                   in1=mk(k), op0=op, op1=ALU.mult).then_inc(s["step"], 1)

            def reduce(m, hf):
                sw = m * 2 + hf
                dve.wait_ge(s["step_used"], (sw + 1) * NT)
                if not isinstance(m, int) or m >= 1:
                    dve.wait_ge(x_ready[L], m if c.split else sw - 1)
                if c.split:
                    src = ps[:, hf * 4 * CH:(hf + 1) * 4 * CH].rearrange("p (q c) -> p q c", q=Q)[:, :, 0:3 * w]
                    nc.vector.tensor_reduce(red[:, hf, 0:Q * w].rearrange("p (q w) -> p q w", q=Q),
                                            src.rearrange("p q (s w) -> p q w s", s=3), AX_X, ALU.add).then_inc(s["reduced"], 1)
                    return
                a0 = (3 * hf + 2) * CH
                srca = ps[:, a0:a0 + CH].rearrange("p (q c) -> p q c", q=Q)[:, :, 0:3 * w]
                nc.vector.tensor_reduce(red_a[:, hf, :].rearrange("p (q w) -> p q w", q=Q),
                                        srca.rearrange("p q (s w) -> p q w s", s=3), AX_X, ALU.add)
                src = ps[:, 3 * hf * CH:(3 * hf + 2) * CH].rearrange("p (q c) -> p q c", q=Q)[:, :, 0:6 * w]
                nc.vector.tensor_reduce(red[:, hf, 0:Q * 2 * w].rearrange("p (q e w) -> p q e w", q=Q, e=2),
                                        src.rearrange("p q (e s w) -> p q e w s", e=2, s=3), AX_X, ALU.add).then_inc(s["reduced"], 1)

            def pair(m):
                dve.wait_ge(s["s_bc_in"], 16 * (m + 1))
                ig = ig_of(L, m)
                dve.wait_ge(s["adjT_in"], 16 * (ig + 1))
                par = held(dve, odd(ig) * (NT * P * 2))
                for hf in range(2):
                    row = s_slot(dve, c, m, hf).rearrange("p (q c) -> p q c", q=Q)
                    d0 = 0 if c.split else held(dve, odd(m) * 8 + hf * 4)
                    g0 = held(dve, (m * 2 + hf) * (NT // RING * A))
                    u0 = held(dve, (m * 2 + hf) * NT)
                    units(row, d0, g0, u0, adjT_masks(par), hf, isinstance(m, int) and m == 0 and hf == 0)
                    if hf == 1:
                        reduce(m, 0)
                    elif not isinstance(m, int):
                        reduce(m - 1, 1)
                    with dve.Fori(1, NT // RING, 1) as j_at:
                        units(row, held(dve, j_at * (RING * H * 4) + d0), held(dve, g0 + j_at * A),
                              held(dve, u0 + j_at * RING), adjT_masks(held(dve, j_at * (RING * P * 2) + par)), hf, False)

            def adjT_masks(tile):
                return lambda k: run(adjT_b, tile + k * P * 2, P, BF16)

            pair(0)
            with dve.Fori(1, NC * c.pairs, 1) as m:
                pair(m)
            reduce(NC * c.pairs - 1, 1)

        def elu_pair(dve, g):
            rows = lambda a, n: a[:, bass.ds(n * Q, Q), :].rearrange("p t d -> p (t d)")
            for parity in range(2):
                o, xv = rows(o_all, g + parity), rows(x_sb, g + parity)
                if v_after(g, 2):
                    dve.wait_ge(tail["y"], g)
                nc.vector.tensor_scalar(s_bc[:, parity * CH:(parity + 1) * CH], o, 0.0, None, ALU.min
                                        ).then_inc(tail["neg"], 1)
                nc.vector.scalar_tensor_tensor(out=xv, in0=o, scalar=0.0, in1=xv, op0=ALU.max, op1=ALU.add
                                               ).then_inc(tail["sum"], 1)
            for parity in range(2):
                xv = rows(x_sb, g + parity)
                dve.wait_ge(tail["exp"], g + parity + 1)
                dve.wait_ge(tail["sum"], g + parity + 1)
                nc.vector.scalar_tensor_tensor(out=xv, in0=s_bc[:, parity * CH:(parity + 1) * CH], scalar=-1.0,
                                               in1=xv, op0=ALU.add, op1=ALU.add).then_inc(tail["y"], 1)

        @block.vector
        def _(dve):
            layer_stats(dve, 0)
            dve.wait_ge(w_turned, 1)
            nc.vector.tensor_copy(w_turn[:, :, :].rearrange("p a b -> p (a b)"), ps[:, 6 * CH:6 * CH + 3 * P]).then_inc(w_copied, 1)
            dve.wait_ge(wa_ready, 1)
            for i, L in enumerate(HEADS):
                w = w_turn[:, 0, :] if i == 0 else w_in[:, i, :]
                nc.vector.tensor_copy(w_ext[L][:, 0:D], w).then_inc(w_done, 1)
                nc.vector.tensor_copy(w_ext[L][:, D:D + 2 * HEADS[L]],
                                      ps[:, 7 * CH + 8 * i:7 * CH + 8 * i + 2 * HEADS[L]]).then_inc(w_done, 1)
            layer_norm(dve, 0)

            def cast(t, parity, ch):
                nc.vector.tensor_scalar(mask[:, parity, ch * CH:(ch + 1) * CH], adj_in[:, parity, ch * CH:(ch + 1) * CH],
                                        0.0, -1.0, ALU.is_gt, ALU.add).then_inc(mask_ready, 1)

            def update(v, parity, last=False):
                dve.wait_ge(p_ready, (v + 1) * NC)
                nc.vector.tensor_reduce(den0[:, parity:parity + 1], row_sum[:, parity, :], AX_X, ALU.add).then_inc(row_step, 1)
                done = 3 * v + 2 - last
                dve.wait_ge(row_step, done + 1)
                nc.vector.reciprocal(rden0[:, parity:parity + 1], den0[:, parity:parity + 1]).then_inc(row_step, 1)
                dve.wait_ge(row_step, done + 2)
                dve.wait_ge(prob_used, (v + 1) * NC)
                xv = x_sb[:, bass.ds(v, 1), :].rearrange("p a d -> p (a d)")
                nc.vector.scalar_tensor_tensor(out=xv, in0=ps[:, 7 * CH:7 * CH + D],
                                               scalar=rden0[:, parity:parity + 1], in1=xv,
                                               op0=ALU.mult, op1=ALU.add).then_inc(x_ready[0], 1)

            def step(t, parity, scores=True, probs=True, upd=True, nxt=True):
                v = t - 1
                first = isinstance(t, int)
                for ch in range(NC + LAG):
                    if nxt and ch < NC:
                        if ch == 0:
                            dve.wait_ge(adj_loaded[1 - parity], 16 * (per(t + 1, 2) + 1))
                        if not first or t >= 1:
                            dve.wait_ge(mt_turned, (t - 1) * NC + ch + 1)
                        if scores:
                            if ch == 0 and (not first or t >= 2):
                                dve.wait_ge(turned, (t - 1) * NC)
                            dve.wait_ge(relu_ready, t * NC + ch + 1)
                        cast(t + 1, 1 - parity, ch)
                    if scores and ch < NC:
                        if not nxt:
                            if ch == 0:
                                dve.wait_ge(turned, (t - 1) * NC)
                            dve.wait_ge(relu_ready, t * NC + ch + 1)
                        nc.vector.tensor_tensor_reduce(
                            out=score[:, parity, ch * CH:(ch + 1) * CH], in0=ps[:, (ch % 4) * CH:(ch % 4 + 1) * CH],
                            in1=relu4[:, ch % 4, :], scale=SLOPE, scalar=-3e38, op0=ALU.add, op1=ALU.max,
                            accum_out=row_max[:, parity, ch:ch + 1]).then_inc(score_ready, 1)
                    if probs and ch >= LAG:
                        cc = ch - LAG
                        nv = v * NC + cc
                        dve.wait_ge(turned, nv + 1)
                        if not first or nv >= 4:
                            dve.wait_ge(prob_used, nv - 3)
                        nc.vector.tensor_copy(prob_T[:, cc % 4, :], ps[:, (5 + cc % 2) * CH:(6 + cc % 2) * CH]).then_inc(prob_ready, 1)
                    if ch == 1 and upd:
                        update(t - 2, parity)
                if scores:
                    dve.wait_ge(score_ready, (t + 1) * NC)
                    if not first or t >= 2:
                        dve.wait_ge(p_ready, (t - 1) * NC)
                    nc.vector.tensor_reduce(row_top[:, parity:parity + 1], row_max[:, parity, :], AX_X, ALU.max).then_inc(row_step, 1)
                    dve.wait_ge(row_step, top_count(t))
                    nc.vector.tensor_scalar(neg_max[:, parity:parity + 1], row_top[:, parity:parity + 1], -1.0, None,
                                            ALU.mult).then_inc(neg_ready, 1)

            def top_count(t):
                return t + 1 if isinstance(t, int) and t < 2 else 3 * t - 1

            dve.wait_ge(adj_loaded[0], 16)
            for ch in range(NC):
                cast(0, 0, ch)
            step(0, 0, probs=False, upd=False)
            step(1, 1, upd=False)
            with dve.Fori(1, NT // 2 - 1, 1) as t_at:
                t = t_at * 2
                step(t, 0)
                step(t + 1, 1)
            step(NT - 2, 0)
            step(NT - 1, 1, nxt=False)
            step(NT, 0, scores=False, nxt=False)
            update(NT - 1, 1, last=True)

            for L in HEADS:
                if L >= layers:
                    break
                layer_stats(dve, L)
                layer_norm(dve, L)
                layer_dve(dve, L)
            if layers == 4:
                dve.wait_ge(x_ready[3], X_DONE[3])
                elu_pair(dve, 0)
                with dve.Fori(1, NC // 2, 1) as g_at:
                    elu_pair(dve, g_at * 2)

        def h_turn(pe, L):
            s = S[L]
            buf = norm0 if L == 0 else norm

            def group(g, parity):
                pe.wait_ge(s["normed"], (g + 1) * Q)
                if not isinstance(g, int) or g >= 2:
                    pe.wait_ge(s["h_done"], g - 1)
                for q in range(Q):
                    last = nc.tensor.transpose(ps[:, parity * CH + q * P:parity * CH + (q + 1) * P],
                                               buf[:, parity, q, :], ident[:, :])
                last.then_inc(s["h_turned"], 1)
                if L:
                    c = Shape(HEADS[L])
                    pe.wait_ge(s["h_done"], g + 1)
                    if not isinstance(g, int) or g >= 2:
                        pe.wait_ge(s["proj_wh"], g - 1)
                        pe.wait_ge(s["s_row_copied"], g - 1)
                    nc.tensor.matmul(ps[0:c.H, (6 + parity) * CH:(7 + parity) * CH], w_ext[L][:, D:D + c.H],
                                     h_grp[:, parity, :], start=True, stop=True).then_inc(s["s_row_turned"], 1)
                    for q in range(Q):
                        at = (2 + 2 * parity) * CH + q * 2 * P
                        last = nc.tensor.matmul(ps[:, at:at + D + 2 * c.H], h_grp[:, parity, q * P:(q + 1) * P],
                                                w_ext[L][:, :], start=True, stop=True, skip_group_check=True)
                    last.then_inc(s["proj"], 1)

            group(0, 0)
            group(1, 1)
            with pe.Fori(1, NC // 2, 1) as g_at:
                g = g_at * 2
                group(g, 0)
                group(g + 1, 1)

        def layer_pe(pe, L):
            s, c = S[L], Shape(HEADS[L])
            w = c.w
            pe.wait_ge(s["table"], NC)
            pe.wait_ge(s["proj_sd"], NC)
            A = len(ON_ACT)

            def units(tab, gi, ni, tile, hf, first):
                for k in range(RING):
                    if k in ON_ACT:
                        pe.wait_ge(s["gate_used"], gi + ON_ACT.index(k) + 1)
                    else:
                        pe.wait_ge(s["step"], ni + ALONE.index(k) + 1)
                    start = first and k == 0
                    if c.split:
                        rows = run(table_b, tab + k * TROW * 2, 3 * w, BF16)
                        for q in range(Q):
                            at = (hf * 4 + q) * CH
                            last = nc.tensor.matmul(ps[:, at:at + 3 * w], steps[:, k, q * P:(q + 1) * P], rows,
                                                    start=start, stop=False, skip_group_check=True)
                    else:
                        rows = run(table_b, tab + k * TROW * 2, 6 * w, BF16)
                        rows_f = run(table_b, tab + (k * TROW + 3 * w) * 2, 3 * w, BF16)
                        for q in range(Q):
                            at = 3 * hf * CH + q * 2 * P
                            nc.tensor.matmul(ps[:, at:at + 6 * w], steps[:, k, q * P:(q + 1) * P], rows,
                                             start=start and q % 2 == 0, stop=False, skip_group_check=True)
                            at = (3 * hf + 2) * CH + q * P
                            mk = run(adjT_b[:, q], tile + k * P * 2, P, BF16)
                            last = nc.tensor.matmul(ps[:, at:at + 3 * w], mk, rows_f,
                                                    start=start and q == 0, stop=False, skip_group_check=True)
                    last.then_inc(s["step_used"], 1)

            ALONE = [k for k in range(RING) if k not in ON_ACT]

            def pair(m):
                ig = ig_of(L, m)
                pe.wait_ge(s["adjT_in"], 16 * (ig + 1))
                par = held(pe, odd(ig) * (NT * P * 2))
                for hf in range(2):
                    sw = m * 2 + hf
                    if not isinstance(sw, int) or sw >= 2:
                        pe.wait_ge(s["reduced"], sw - 1)
                    t0 = hf * 6 * w if c.split else held(pe, odd(m) * (24 * w) + hf * 12 * w)
                    g0 = held(pe, sw * (NT // RING * A))
                    n0 = held(pe, sw * (NT // RING * (RING - A)))
                    units(t0, g0, n0, par, hf, True)
                    with pe.Fori(1, NT // RING, 1) as j_at:
                        units(held(pe, j_at * (RING * TROW * 2) + t0), held(pe, g0 + j_at * A),
                              held(pe, n0 + j_at * (RING - A)), held(pe, j_at * (RING * P * 2) + par), hf, False)

            pair(0)
            with pe.Fori(1, NC * c.pairs, 1) as m:
                pair(m)

        @block.tensor
        def _(pe):
            pe.wait_ge(set_up, 8)
            pe.wait_ge(loaded["ks"], 16)
            for g in range(NC):
                if g >= 2:
                    pe.wait_ge(ks_copied, g - 1)
                for q in range(Q):
                    last = nc.tensor.transpose(ps[:, (g % 2) * CH + q * P:(g % 2) * CH + (q + 1) * P],
                                               ks_nat[:, g * Q + q, :], ident[:, :])
                last.then_inc(ks_turned, 1)
            pe.wait_ge(loaded["w"], 48)
            for i in range(3):
                last = nc.tensor.transpose(ps[:, 6 * CH + i * P:6 * CH + (i + 1) * P], w_in[:, i, :], ident[:, :])
            last.then_inc(w_turned, 1)
            pe.wait_ge(w_copied, 1)
            pe.wait_ge(loaded["a"], 16 * 18)
            for i in range(3):
                w = w_in[:, 0, :] if i == 0 else w_turn[:, i, :]
                last = nc.tensor.matmul(ps[:, 7 * CH + 8 * i:7 * CH + 8 * i + 8], w, a_blk[:, i, :], start=True, stop=True,
                                        skip_group_check=True)
            last.then_inc(wa_ready, 1)
            pe.wait_ge(ks_copied, NC)
            h_turn(pe, 0)
            pe.wait_ge(S[0]["h_done"], NC)
            pe.wait_ge(w_done, 6)

            def step(t, parity, scores=True, probs=True):
                v, vp = t - 1, 1 - parity
                first = isinstance(t, int)
                for ch in range(NC + LAG + 1):
                    if scores and ch < NC:
                        n = t * NC + ch
                        if ch == 0:
                            pe.wait_ge(h_tile_ready, t + 1)
                        if not first or n >= 4:
                            pe.wait_ge(score_ready, n - 3)
                        pe.wait_ge(mask_ready, n + 1)
                        bank = ps[:, (ch % 4) * CH:(ch % 4 + 1) * CH]
                        nc.tensor.matmul(bank, h_tile[:, parity, :], ks_T[:, ch * CH:(ch + 1) * CH], start=True, stop=False)
                        nc.tensor.matmul(bank, big_ident[:, :], mask[:, parity, ch * CH:(ch + 1) * CH],
                                         start=False, stop=True).then_inc(s_ready, 1)
                        if not first or n >= 1:
                            pe.wait_ge(mt_copied, n)
                        for q in range(Q):
                            at = 4 * 2 * CH + q * P
                            last = nc.tensor.transpose(ps_b[:, at:at + P],
                                                       mask[:, parity, ch * CH + q * P:ch * CH + (q + 1) * P], identb[:, :])
                        last.then_inc(mt_turned, 1)
                    if probs and LAG <= ch < NC + LAG:
                        cc = ch - LAG
                        nv = v * NC + cc
                        pe.wait_ge(p_ready, nv + 1)
                        if not first or nv >= 2:
                            pe.wait_ge(prob_ready, nv - 1)
                        for q in range(Q):
                            at = (5 + cc % 2) * CH + q * P
                            last = nc.tensor.transpose(ps[:, at:at + P],
                                                       score[:, vp, cc * CH + q * P:cc * CH + (q + 1) * P], ident[:, :])
                        last.then_inc(turned, 1)
                    if probs and ch > LAG:
                        cc = ch - LAG - 1
                        nv = v * NC + cc
                        pe.wait_ge(prob_ready, nv + 1)
                        if cc == 0 and (not first or v >= 1):
                            pe.wait_ge(x_ready[0], v)
                        for q in range(Q):
                            last = nc.tensor.matmul(ps[:, 7 * CH:7 * CH + D],
                                                    prob_T[:, cc % 4, q * P:(q + 1) * P], ks_nat[:, cc * Q + q, :],
                                                    start=(cc == 0 and q == 0), stop=(cc == NC - 1 and q == Q - 1),
                                                    skip_group_check=True)
                        last.then_inc(prob_used, 1)

            step(0, 0, probs=False)
            step(1, 1)
            with pe.Fori(1, NT // 2, 1) as t_at:
                t = t_at * 2
                step(t, 0)
                step(t + 1, 1)
            step(NT, 0, scores=False)

            for L in HEADS:
                if L >= layers:
                    break
                pe.wait_ge(x_ready[L - 1], X_DONE[L - 1])
                h_turn(pe, L)
                layer_pe(pe, L)


_INS = ["x", "adj", "L0_gnn_ks", "L1_gnn_W", "L1_gnn_attn_src", "L1_gnn_attn_dst", "L2_gnn_W", "L2_gnn_a",
        "L3_gnn_W", "L3_gnn_a"]
LAYERS = 4


def kernel(**inputs):
    import numpy as _np
    import concourse.bacc as _bacc
    from concourse import mybir as _mybir
    from concourse.bass_utils import run_bass_kernel_spmd as _run

    nc = _bacc.Bacc("TRN2", target_bir_lowering=False, num_devices=1)
    arrays, args = {}, []
    for name in _INS:
        a = _np.ascontiguousarray(inputs[name])
        arrays[f"in_{name}_dram"] = a
        args.append(nc.dram_tensor(f"in_{name}_dram", a.shape, _mybir.dt.from_np(a.dtype), kind="ExternalInput").ap())
    args.append(nc.dram_tensor("out_0_dram", (N, D), F32, kind="ExternalOutput").ap())
    bass_gnn_stack_kernel(nc, *args, layers=LAYERS)
    r = _run(nc, [arrays], core_ids=[0])
    return r.results[0]["out_0_dram"]
```

```python
from contextlib import ExitStack

import concourse.bass as bass
from concourse import mybir

F32 = mybir.dt.float32
BF16 = mybir.dt.bfloat16
I32 = mybir.dt.int32
U8 = mybir.dt.uint8
BYTES = {F32: 4, I32: 4, BF16: 2, U8: 1}
ALU = mybir.AluOpType
ACT = mybir.ActivationFunctionType
AX_X = mybir.AxisListType.X
RMAX = bass.bass_isa.ReduceOp.max

N, D, P = 4096, 128, 128
NT = N // P
CH = 512
NC = N // CH
Q = CH // P
EPS = 1e-5
SLOPE = 0.2
BIG = 2.0 ** 100
STEEP = 1e30
RING = 8
ON_ACT = [k for k in range(NT) if k % 16 not in (2, 5, 8, 11, 14)]
ALONE = [k for k in range(NT) if k not in ON_ACT]
GATES = len(ON_ACT) // 2
REDUCE_AT = 10
LAG = 2

HEADS = {1: 4, 2: 1, 3: 4}


def per(a, b):
    return a // b


def v_after(a, least):
    return not isinstance(a, int) or a >= least


def held(eng, a):
    return a if isinstance(a, int) else eng.snap(a)


def odd(a):
    return a % 2 if isinstance(a, int) else a & 1


class Shape:

    def __init__(self, heads):
        self.H = heads
        self.dh = D // heads
        self.w = self.dh + 1
        self.row = heads * 2 * 3 * self.w
        self.pairs = 2 if heads > 1 else 1
        self.split = heads == 1


def bass_gnn_stack_kernel(nc, x, adj, ks, w1, a1_src, a1_dst, w2, a2, w3, a3, out, layers=4):
    ctx = ExitStack()
    with ctx:
        top = [(nc.sbuf_base + 31) // 32 * 32]

        def place(name, shape, dtype, at=None):
            size = 1
            for n in shape[1:]:
                size *= n
            size *= BYTES[dtype]
            if at is None:
                at = top[0]
                top[0] = (at + size + 31) // 32 * 32
            return nc.alloc_sbuf_tensor_at(name, shape, dtype, offset=at)

        def place_bytes(name, shape, dtype):
            b = place(name, shape[:-1] + [shape[-1] * BYTES[dtype]], U8)
            return b, b[(slice(None),) * len(shape)].bitcast(dtype)

        def run(view, at, n, dtype):
            return view[(slice(None),) * (len(view.shape) - 1) + (bass.ds(at, n * BYTES[dtype]),)].bitcast(dtype)

        def sem(name):
            return ctx.enter_context(nc.semaphore(name))

        x_sb = place("x_sb", [P, NT, D], F32)
        ident = place("ident", [P, P], F32)
        identb = place("identb", [P, P], BF16)
        big_ident = place("big_ident", [P, P], BF16)
        ones_col = place("ones_col", [P, 1], F32)
        minus_half = place("minus_half", [P, NT], F32)
        minus_one = place("minus_one", [P, Q], F32)
        w_ext = {L: place(f"w_ext{L}", [P, D + 2 * HEADS[L]], F32) for L in HEADS}
        stats = place("stats", [P, NT, 6], F32)
        mean = place("mean", [P, NT], F32)
        rstd = place("rstd", [P, NT], F32)
        st_tmp = place("st_tmp", [P, 5, NT], F32)
        phase = top[0]

        ks_T = place("ks_T", [P, N], F32)
        ks_nat = place("ks_nat", [P, NT, D], F32)
        adj_in = place("adj_in", [P, 2, N], I32)
        mask = place("mask", [P, 2, N], BF16)
        relu4 = place("relu4", [P, 4, CH], F32)
        score = place("score", [P, 2, N], F32)
        prob_T = place("prob_T", [P, 4, CH], F32)
        adjT_out = place("adjT_out", [P, 2, NT, P], BF16)
        h_T = place("h_T", [P, N], F32)
        h_tile = place("h_tile", [P, 2, P], F32)
        norm0 = place("norm0", [P, 2, Q, D], F32)
        row_max = place("row_max", [P, 2, NC], F32)
        row_top = place("row_top", [P, 2], F32)
        neg_max = place("neg_max", [P, 2], F32)
        row_sum = place("row_sum", [P, 2, NC], F32)
        den0 = place("den0", [P, 2], F32)
        rden0 = place("rden0", [P, 2], F32)
        w_in = place("w_in", [P, 3, P], F32)
        w_turn = place("w_turn", [P, 3, P], F32)
        a_blk = place("a_blk", [P, 3, 8], F32)

        top[0] = phase
        TROW = max(Shape(h).row for h in HEADS.values())
        WMAX = max(Shape(h).w for h in HEADS.values())
        table_b, table = place_bytes("table", [P, NT * TROW], BF16)
        adjT_b, adjT = place_bytes("adjT", [P, Q, 2 * NT * P], BF16)
        s_bc_b, s_bc = place_bytes("s_bc", [P, 4 * CH], F32)
        at = top[0]
        norm = place("norm", [P, 2, Q, D], F32)
        h_grp = place("h_grp", [P, 2, CH], F32)
        after = top[0]
        top[0] = at
        steps = place("steps", [P, RING, CH], BF16)
        gates = place("gates", [P, GATES, CH], BF16)
        top[0] = max(top[0], after)
        at = top[0]
        prod = place("prod", [P, 2, 1056], F32)
        rest = place("rest", [P, 2, 1056], F32)
        after = top[0]
        top[0] = at
        red = place("red", [P, 2, 2 * Q * WMAX], F32)
        red_a = place("red_a", [P, Q * 2 * 33], F32)
        pt = [place(f"pt{i}", [P, Q * WMAX], F32) for i in range(3)]
        assert top[0] <= after
        top[0] = after
        at = top[0]
        wh = place("wh", [P, NT, D], F32)
        o_all = place("o_all", [P, NT, D], F32, at=at)
        s_row = place("s_row", [4, 2, CH], F32)
        sd = place("sd", [P, NT, 8], F32)
        d_max = place("d_max", [P, 4], F32)
        d_top = place("d_top", [P, 4], F32)
        d_rel = place("d_rel", [P, NT * 4], F32)
        s_lim = place("s_lim", [P, 2, NT * 4], F32)
        s_top = place("s_top", [P, NT * 4], F32)
        ef = place("ef", [P, 2, NT * 4], F32)
        ab = place("ab", [P, 2, NT * 4], F32)
        neg_d_b, neg_d = place_bytes("neg_d", [P, NT * 4], F32)
        steep_b, steep_d = place_bytes("steep_d", [P, 2, NT * 4], F32)
        rden = place("rden", [P, Q], F32)
        assert top[0] <= nc.sbuf_usable_end, top[0]

        ps = ctx.enter_context(nc.psum_tensor("ps", [P, 8 * CH], F32))
        ps_b = ps[:, :].bitcast(BF16)

        adjT_d = nc.dram_tensor("adjT_d", [NT, P, NT * P], BF16).ap()
        s_d = {L: nc.dram_tensor(f"s_d{L}", [HEADS[L], N], F32).ap() for L in HEADS}

        loaded = {n: sem(f"loaded_{n}") for n in ("x", "ks", "w", "a")}
        set_up = sem("set_up")
        w_turned = sem("w_turned")
        w_copied = sem("w_copied")
        wa_ready = sem("wa_ready")
        w_done = sem("w_done")
        ks_turned = sem("ks_turned")
        ks_copied = sem("ks_copied")
        adj_loaded = [sem("adj_loaded0"), sem("adj_loaded1")]
        mask_ready = sem("mask_ready")
        h_tile_ready = sem("h_tile_ready")
        s_ready = sem("s_ready")
        relu_ready = sem("relu_ready")
        score_ready = sem("score_ready")
        neg_ready = sem("neg_ready")
        p_ready = sem("p_ready")
        turned = sem("turned")
        prob_ready = sem("prob_ready")
        prob_used = sem("prob_used")
        mt_turned = sem("mt_turned")
        mt_copied = sem("mt_copied")
        adjT_stored = [sem("adjT_stored0"), sem("adjT_stored1")]
        x_ready = {L: sem(f"x_ready{L}") for L in range(4)}
        row_step = sem("row_step")
        stored = sem("stored")

        block = ctx.enter_context(nc.Block())

        ig_of = lambda L, m: per(m, Shape(HEADS[L]).pairs)
        S = {}
        for L in [0] + list(HEADS):
            names = ["stat", "stat_step", "var", "rstd", "normed", "h_turned", "h_done"]
            if L:
                names += ["proj", "proj_wh", "proj_sd", "s_row_turned", "s_row_copied", "d_max", "d_top", "s_top",
                          "rel", "ef", "neg", "prod", "prod1", "ones", "hi", "r1", "mid", "table", "s_stored0", "s_stored1",
                          "adjT_in", "s_bc_in", "gate", "gate_used", "step", "step_used", "reduced", "pool_step"]
            S[L] = {n: sem(f"L{L}_{n}") for n in names}
        tail = {n: sem(f"tail_{n}") for n in ("neg", "exp", "sum", "y")}
        X_DONE = {0: NT, 1: 32, 2: 8, 3: 32}

        def layer0_stored(eng):
            for done in adjT_stored:
                eng.wait_ge(done, 16 * NT // 2)

        def adjT_half(c, m, parity, hf):
            if c.split:
                return parity * (NT * P * 2)
            return per(m, 2) % 2 * (NT * P * 2) if hf else (m & 2) * (NT * P)

        def each_pair(eng, c, pair):
            last = NC * c.pairs - 1
            pair(0, 0)
            with eng.Fori(1, NC * c.pairs // 2, 1) as at:
                pair(at * 2 - 1, 1)
                pair(at * 2, 0)
            pair(last, 1)

        def layer_dma(sp, L):
            s, c = S[L], Shape(HEADS[L])

            def load_adjT(ig, parity):
                sp.dma_start(adjT[:, :, parity * NT * P:(parity + 1) * NT * P],
                             adjT_d[bass.ds(ig * Q, Q)].rearrange("q p c -> p q c")).then_inc(s["adjT_in"], 16)

            def load_s(m):
                ig = ig_of(L, m)
                if c.split:
                    rows, slot, n = 0, odd(m), 1
                else:
                    rows, slot, n = odd(m) * 2, odd(m) * 2, 2
                src = s_d[L][bass.ds(rows, n), bass.ds(ig * CH, CH)]
                sp.dma_start(s_bc[:, bass.ds(slot * CH, n * CH)].rearrange("p (h c) -> p h c", h=n), src.partition_broadcast(P)).then_inc(s["s_bc_in"], 16)

            sp.wait_ge(x_ready[L - 1], X_DONE[L - 1])
            load_adjT(0, 0)
            with sp.Fori(0, NC // 2, 1) as g_at:
                g = g_at * 2
                for parity in range(2):
                    sp.wait_ge(s["s_row_copied"], g + parity + 1)
                    sp.dma_start(s_d[L][:, bass.ds((g + parity) * CH, CH)],
                                 s_row[0:c.H, parity, :]).then_inc(s[f"s_stored{parity}"], 16)
            for parity in range(2):
                sp.wait_ge(s[f"s_stored{parity}"], 16 * NC // 2)
            load_s(0)
            sp.wait_ge(s["s_bc_in"], 16)
            load_s(1)
            sp.wait_ge(s["table"], NC)
            sp.wait_ge(s["adjT_in"], 16)
            load_adjT(1, 1)

            def next_s(m):
                sp.wait_ge(s["gate_used"], 2 * (m + 1) * len(ON_ACT))
                sp.wait_ge(s["s_bc_in"], 16 * (m + 2))
                load_s(m + 2)

            with sp.Fori(0, NC // 2 - 1, 1) as ig_at:
                for parity in range(2):
                    ig = ig_at * 2 + parity
                    for pp in range(c.pairs):
                        next_s(ig * c.pairs + pp)
                    sp.wait_ge(s["step_used"], (ig + 1) * 2 * c.pairs * NT)
                    sp.wait_ge(s["adjT_in"], 16 * (ig + 2))
                    load_adjT(ig + 2, parity)
            for m in range((NC - 2) * c.pairs, NC * c.pairs - 2):
                next_s(m)

        @block.sync
        def _(sp):
            sp.dma_start(x_sb[:, :, :], x.rearrange("(t p) d -> p t d", p=P)).then_inc(loaded["x"], 16)
            sp.dma_start(ks_nat[:, :, :], ks.rearrange("(t p) d -> p t d", p=P)).then_inc(loaded["ks"], 16)

            def load_adj(t, parity):
                sp.dma_start(adj_in[:, parity, :], adj_tiles(t)).then_inc(adj_loaded[parity], 16)

            def adj_tiles(t):
                return adj[bass.ds(t * P, P), :]

            load_adj(0, 0)
            for i, w in enumerate((w1, w2, w3)):
                sp.dma_start(w_in[:, i, :], w).then_inc(loaded["w"], 16)
            sp.wait_ge(set_up, 5)
            n = 0
            for h in range(4):
                rows = slice(32 * h, 32 * h + 32)
                for src, i, col in ((a1_src[0, h], 0, h), (a1_dst[0, h], 0, 4 + h),
                                    (a3[0, h, 0:32], 2, h), (a3[0, h, 32:64], 2, 4 + h)):
                    sp.dma_start(a_blk[rows, i, col:col + 1], src.unsqueeze(1)).then_inc(loaded["a"], 16)
                    n += 1
            for k in range(2):
                sp.dma_start(a_blk[:, 1, k:k + 1], a2[k * D:(k + 1) * D, :]).then_inc(loaded["a"], 16)
                n += 1
            assert n == 18
            load_adj(1, 1)

            def step(t, parity, more=True):
                if more:
                    sp.wait_ge(mask_ready, (t + 1) * NC)
                    load_adj(t + 2, parity)
                sp.wait_ge(mt_copied, (t + 1) * NC)
                sp.dma_start(adjT_d[bass.ds(t, 1)].rearrange("a p c -> (a p) c"),
                             adjT_out[:, parity].rearrange("p t c -> p (t c)")).then_inc(adjT_stored[parity], 16)

            with sp.Fori(0, NT // 2 - 1, 1) as t_at:
                t = t_at * 2
                step(t, 0)
                step(t + 1, 1)
            step(NT - 2, 0, more=False)
            step(NT - 1, 1, more=False)
            layer0_stored(sp)

            for L in HEADS:
                if L >= layers:
                    break
                layer_dma(sp, L)
            if layers < 4:
                sp.wait_ge(x_ready[layers - 1], X_DONE[layers - 1])
                sp.dma_start(out.rearrange("(t p) d -> p t d", p=P), x_sb[:, :, :]).then_inc(stored, 16)
                sp.wait_ge(stored, 16)
            else:
                with sp.Fori(0, NC, 1) as g:
                    sp.wait_ge(tail["y"], g + 1)
                    sp.dma_start(out[bass.ds(g * CH, CH), :].rearrange("(t p) d -> p t d", p=P),
                                 x_sb[:, bass.ds(g * Q, Q), :]).then_inc(stored, 16)
                sp.wait_ge(stored, 16 * NC)

        def rstd_pow(pool, L):
            s = S[L]
            pool.wait_ge(s["var"], 1)
            nc.gpsimd.tensor_tensor(rstd[:, :], st_tmp[:, 4, :], minus_half[:, :], ALU.pow).then_inc(s["rstd"], 1)

        def layer_pool(pool, L):
            s, c = S[L], Shape(HEADS[L])
            H, dh, w = c.H, c.dh, c.w
            pool.wait_ge(s["d_max"], 1)
            nc.gpsimd.partition_all_reduce(d_top[:, 0:H], d_max[:, 0:H], P, RMAX).then_inc(s["d_top"], 1)

            def table_part(g, parity):
                pv = prod[:, parity, 0:Q * H * 2 * w].rearrange("p (t h e w) -> p t h e w", t=Q, h=H, e=2)
                efv = ef[:, :, 0:NT * H].rearrange("p e (t h) -> p e t h", h=H)
                pool.wait_ge(s["ef"], 2)
                if not isinstance(g, int) or g >= 2:
                    pool.wait_ge(s["r1"], g - 1)
                for e in range(2):
                    last = nc.gpsimd.tensor_copy(pv[:, :, :, e, dh], efv[:, e, bass.ds(g * Q, Q), :]
                                                 ).then_inc(s["ones"], 1)
                pool.wait_ge(s["ones"], 2 * (g + 1))
                nc.gpsimd.tensor_tensor(
                    pv[:, :, :, 1, 0:dh],
                    wh[:, bass.ds(g * Q, Q), :].rearrange("p t (h d) -> p t h d", h=H),
                    efv[:, 1, bass.ds(g * Q, Q), :].unsqueeze(3).to_broadcast([P, Q, H, dh]),
                    ALU.mult).then_inc(s["prod1"], 1)

            table_part(0, 0)
            table_part(1, 1)
            with pool.Fori(1, NC // 2, 1) as g_at:
                g = g_at * 2
                table_part(g, 0)
                table_part(g + 1, 1)

            view = lambda a: a[:, 0:Q * w].rearrange("p (q w) -> p q w", q=Q)
            ta, tb, tc = (view(a) for a in pt)

            def combine(n, ig, h, e_sum, f_sum, a_sum):
                base = n * KSTEP
                k = [0]

                def wait():
                    pool.wait_ge(s["pool_step"], base + k[0])

                def done(ins):
                    k[0] += 1
                    ins.then_inc(s["pool_step"], 1)

                abv = ab[:, :, 0:NT * H].rearrange("p e (t h) -> p e t h", h=H)

                def factor(e, width):
                    return abv[:, e, bass.ds(ig * Q, Q), bass.ds(h, 1)].to_broadcast([P, Q, width])

                if not c.split:
                    done(nc.gpsimd.tensor_tensor(tb, a_sum, f_sum, ALU.subtract))
                    wait()
                    f_sum = tb
                done(nc.gpsimd.tensor_tensor(tc, f_sum, factor(1, w), ALU.mult))
                done(nc.gpsimd.tensor_tensor(ta, e_sum, factor(0, w), ALU.mult))
                wait()
                done(nc.gpsimd.tensor_tensor(tb, ta, tc, ALU.add))
                wait()
                done(nc.gpsimd.tensor_tensor(rden[:, :], tb[:, :, dh], minus_one[:, :], ALU.pow))
                wait()
                rb = rden[:, :].unsqueeze(2).to_broadcast([P, Q, dh])
                cols = bass.ds(h * dh, dh)
                if L == 3:
                    nc.gpsimd.tensor_tensor(o_all[:, bass.ds(ig * Q, Q), cols], tb[:, :, 0:dh], rb, ALU.mult
                                            ).then_inc(x_ready[L], 1)
                else:
                    done(nc.gpsimd.tensor_tensor(ta[:, :, 0:dh], tb[:, :, 0:dh], rb, ALU.mult))
                    wait()
                    xv = x_sb[:, bass.ds(ig * Q, Q), cols]
                    nc.gpsimd.tensor_tensor(xv, xv, ta[:, :, 0:dh], ALU.add).then_inc(x_ready[L], 1)
                pool.wait_ge(x_ready[L], n + 1)
                assert k[0] == KSTEP

            KSTEP = (4 if c.split else 5) + (L != 3)

            with pool.Fori(0, NC * c.pairs, 1) as m:
                ig = ig_of(L, m)
                if c.split:
                    pool.wait_ge(s["reduced"], 2 * (m + 1))
                    combine(m, ig, 0, view(red[:, 0]), view(red[:, 1]), None)
                else:
                    pool.wait_ge(s["reduced"], 2 * (m + 1))
                    for hf in range(2):
                        n = m * 2 + hf
                        rv = red[:, hf, 0:Q * 2 * w].rearrange("p (q e w) -> p q e w", q=Q, e=2)
                        combine(n, ig, odd(m) * 2 + hf, rv[:, :, 0, :], rv[:, :, 1, :], 
                                red_a[:, 0:Q * 2 * w].rearrange("p (q h w) -> p q h w", q=Q, h=2)[:, :, hf, :])

        @block.gpsimd
        def _(pool):
            nc.gpsimd.memset(ident[:, :], 0.0).then_inc(set_up, 1)
            nc.gpsimd.memset(ones_col[:, :], 1.0).then_inc(set_up, 1)
            nc.gpsimd.memset(minus_half[:, :], -0.5).then_inc(set_up, 1)
            nc.gpsimd.memset(a_blk[:, :, :], 0.0).then_inc(set_up, 1)
            nc.gpsimd.memset(minus_one[:, :], -1.0).then_inc(set_up, 1)
            pool.wait_ge(set_up, 5)
            nc.gpsimd.affine_select(out=ident[:, :], in_=ident[:, :], compare_op=ALU.not_equal, fill=1.0,
                                    base=0, pattern=[[-1, P]], channel_multiplier=1).then_inc(set_up, 1)
            pool.wait_ge(set_up, 6)
            nc.gpsimd.tensor_copy(identb[:, :], ident[:, :]).then_inc(set_up, 1)
            nc.gpsimd.tensor_scalar(big_ident[:, :], ident[:, :], BIG, 0.0, ALU.mult, ALU.add).then_inc(set_up, 1)

            rstd_pow(pool, 0)

            def step(t, parity):
                pool.wait_ge(s_ready, t * NC)
                nc.gpsimd.tensor_copy(h_tile[:, 1 - parity, :], h_T[:, bass.ds((t + 1) * P, P)]
                                      ).then_inc(h_tile_ready, 1)

            pool.wait_ge(S[0]["h_done"], NC)
            nc.gpsimd.tensor_copy(h_tile[:, 0, :], h_T[:, 0:P]).then_inc(h_tile_ready, 1)
            step(0, 0)
            with pool.Fori(0, NT // 2 - 1, 1) as t_at:
                t = t_at * 2 + 1
                step(t, 1)
                step(t + 1, 0)

            for L in HEADS:
                if L >= layers:
                    break
                rstd_pow(pool, L)
                layer_pool(pool, L)

        def h_relu(act, L):
            s = S[L]
            if L == 1:
                layer0_stored(act)

            def group(g, parity):
                act.wait_ge(s["h_turned"], g + 1)
                if L == 0:
                    dst = h_T[:, bass.ds(g * CH, CH)]
                else:
                    dst = h_grp[:, parity, :]
                    if not isinstance(g, int) or g >= 2:
                        act.wait_ge(s["proj"], g - 1)
                nc.scalar.activation(dst, ps[:, parity * CH:(parity + 1) * CH], ACT.Relu).then_inc(s["h_done"], 1)
                if L:
                    act.wait_ge(s["proj"], g + 1)
                    src = ps[:, (2 + 2 * parity) * CH:(4 + 2 * parity) * CH].rearrange("p (q c) -> p q c", q=Q)
                    nc.scalar.copy(wh[:, bass.ds(g * Q, Q), :], src[:, :, 0:D]).then_inc(s["proj_wh"], 1)

            group(0, 0)
            group(1, 1)
            with act.Fori(1, NC // 2, 1) as g_at:
                g = g_at * 2
                group(g, 0)
                group(g + 1, 1)

        def layer_act(act, L):
            s, c = S[L], Shape(HEADS[L])
            H, w = c.H, c.w
            n = NT * H
            h_relu(act, L)
            act.wait_ge(s["rel"], 1)
            nc.scalar.activation(ef[:, 0, 0:n], d_rel[:, 0:n], ACT.Exp).then_inc(s["ef"], 1)
            nc.scalar.activation(ef[:, 1, 0:n], d_rel[:, 0:n], ACT.Exp, scale=SLOPE).then_inc(s["ef"], 1)
            act.wait_ge(s["rel"], 3)
            nc.scalar.activation(ab[:, :, 0:n], s_lim[:, :, 0:n], ACT.Exp).then_inc(s["ef"], 1)

            def table_part(g, parity):
                act.wait_ge(s["prod"], g + 1)
                act.wait_ge(s["prod1"], g + 1)
                nc.scalar.copy(table_view(g, 0, c), prod_view(prod, parity, c)).then_inc(s["hi"], 1)
                act.wait_ge(s["r1"], g + 1)
                nc.scalar.copy(table_view(g, 1, c), prod_view(rest, parity, c)).then_inc(s["mid"], 1)

            with act.Fori(0, NC // 2, 1) as g_at:
                g = g_at * 2
                table_part(g, 0)
                table_part(g + 1, 1)

            act.wait_ge(s["neg"], 3 if c.split else 2)

            def sweep(row, h, gi, sw, flip):
                for i, k in enumerate(ON_ACT):
                    if v_after(sw, 1) or i >= GATES:
                        act.wait_ge(s["gate_used"], gi + i + 1 - GATES)
                    at = h + k * H
                    nc.scalar.activation(gates[:, i % GATES, :], row, ACT.Sigmoid,
                                         bias=steep_d[:, 1 if flip else 0, at:at + 1],
                                         scale=-STEEP if flip else STEEP).then_inc(s["gate"], 1)

            def pair(m, parity):
                act.wait_ge(s["s_bc_in"], 16 * (m + 1))
                for hf in range(2):
                    sw = m * 2 + hf
                    sweep(s_row_of(c, parity, hf), head_of(c, parity, hf), held(act, sw * len(ON_ACT)), sw, c.split and hf)

            each_pair(act, c, pair)

        def head_of(c, parity, hf):
            return 0 if c.split else parity * 2 + hf

        def s_row_of(c, parity, hf):
            slot = parity if c.split else parity * 2 + hf
            return s_bc[:, slot * CH:(slot + 1) * CH]

        def table_view(g, part, c):
            t = table[:, :].rearrange("p (t r) -> p t r", t=NT)[:, bass.ds(g * Q, Q), 0:c.row]
            return t.rearrange("p t (b s w) -> p t b s w", s=3, w=c.w)[:, :, :, part, :]

        def prod_view(b, parity, c):
            return b[:, parity, 0:Q * c.H * 2 * c.w].rearrange("p (t b w) -> p t b w", t=Q, w=c.w)

        @block.scalar
        def _(act):
            for g in range(NC):
                act.wait_ge(ks_turned, g + 1)
                nc.scalar.copy(ks_T[:, g * CH:(g + 1) * CH], ps[:, (g % 2) * CH:(g % 2 + 1) * CH]).then_inc(ks_copied, 1)
            h_relu(act, 0)
            act.wait_ge(set_up, 8)

            def step(t, parity, scores=True, probs=True):
                v, vp = t - 1, 1 - parity
                first = isinstance(t, int)
                for ch in range(NC):
                    if probs:
                        nv = v * NC + ch
                        if ch == 0:
                            act.wait_ge(neg_ready, v + 1)
                            if v_after(v, 1):
                                act.wait_ge(row_step, 3 * v - 2)
                        sl = score[:, vp, ch * CH:(ch + 1) * CH]
                        nc.scalar.activation(sl, sl, ACT.Exp, bias=neg_max[:, vp:vp + 1],
                                             accum_out=row_sum[:, vp, ch:ch + 1]).then_inc(p_ready, 1)
                    if scores:
                        n = t * NC + ch
                        act.wait_ge(s_ready, n + 1)
                        if not first or n >= 4:
                            act.wait_ge(score_ready, n - 3)
                        nc.scalar.activation(relu4[:, ch % 4, :], ps[:, (ch % 4) * CH:(ch % 4 + 1) * CH], ACT.Relu,
                                             scale=1.0 / SLOPE - 1.0).then_inc(relu_ready, 1)
                        act.wait_ge(mt_turned, n + 1)
                        if ch == 0 and (not first or t >= 2):
                            act.wait_ge(adjT_stored[parity], 16 * per(t, 2))
                        mt = ps_b[:, 4 * 2 * CH:4 * 2 * CH + CH]
                        nc.scalar.activation(adjT_out[:, parity, ch * Q:(ch + 1) * Q, :].rearrange("p t c -> p (t c)"),
                                             mt, ACT.Identity, bias=ones_col[:, 0:1]).then_inc(mt_copied, 1)

            step(0, 0, probs=False)
            step(1, 1)
            with act.Fori(1, NT // 2, 1) as t_at:
                t = t_at * 2
                step(t, 0)
                step(t + 1, 1)
            step(NT, 0, scores=False)

            for L in HEADS:
                if L >= layers:
                    break
                layer_act(act, L)
            if layers == 4:
                with act.Fori(0, NC // 2, 1) as g_at:
                    g = g_at * 2
                    for parity in range(2):
                        act.wait_ge(tail["neg"], g + parity + 1)
                        v = s_bc[:, parity * CH:(parity + 1) * CH]
                        nc.scalar.activation(v, v, ACT.Exp).then_inc(tail["exp"], 1)

        def layer_stats(dve, L):
            s = S[L]
            if L == 0:
                dve.wait_ge(loaded["x"], 16)
            else:
                dve.wait_ge(x_ready[L - 1], X_DONE[L - 1])
            if L == 1:
                layer0_stored(dve)
            with dve.Fori(0, NT // 4, 1) as t_at:
                t = t_at * 4
                for k in range(4):
                    nc.vector.bn_stats(stats[:, bass.ds(t + k, 1), :].rearrange("p a b -> p (a b)"),
                                       x_sb[:, bass.ds(t + k, 1), :].rearrange("p a b -> p (a b)")).then_inc(s["stat"], 1)
            dve.wait_ge(s["stat"], NT)
            k = [0]

            def link(ins):
                k[0] += 1
                ins.then_inc(s["stat_step"], 1)
                dve.wait_ge(s["stat_step"], k[0])

            me, mo, ve, vo = (stats[:, :, i] for i in (1, 4, 2, 5))
            t0, t1, t2, t3, veps = (st_tmp[:, i, :] for i in range(5))
            link(nc.vector.tensor_tensor(t0, me, mo, ALU.add))
            link(nc.vector.tensor_tensor(t1, me, mo, ALU.subtract))
            link(nc.vector.tensor_tensor(t2, ve, vo, ALU.add))
            link(nc.vector.scalar_tensor_tensor(out=t3, in0=t1, scalar=0.25, in1=t1, op0=ALU.mult, op1=ALU.mult))
            link(nc.vector.tensor_scalar(mean[:, :], t0, 0.5, None, ALU.mult))
            link(nc.vector.tensor_scalar(t2, t2, 1.0 / D, EPS, ALU.mult, ALU.add))
            nc.vector.tensor_tensor(veps, t2, t3, ALU.add).then_inc(s["var"], 1)

        def layer_norm(dve, L):
            s = S[L]
            buf = norm0 if L == 0 else norm
            dve.wait_ge(s["rstd"], 1)

            def group(g, parity):
                if not isinstance(g, int) or g >= 2:
                    dve.wait_ge(s["h_turned"], g - 1)
                for q in range(Q):
                    t = g * Q + q
                    nc.vector.tensor_scalar(buf[:, parity, q, :], x_sb[:, bass.ds(t, 1), :].rearrange("p a b -> p (a b)"),
                                            mean[:, bass.ds(t, 1)], rstd[:, bass.ds(t, 1)],
                                            ALU.subtract, ALU.mult).then_inc(s["normed"], 1)
                if L and (not isinstance(g, int) or g >= 1):
                    after_projection(g - 1, 1 - parity)

            def after_projection(g, parity):
                c = Shape(HEADS[L])
                dve.wait_ge(s["proj_wh"], g + 1)
                src = ps[:, (2 + 2 * parity) * CH:(4 + 2 * parity) * CH].rearrange("p (q c) -> p q c", q=Q)
                nc.vector.tensor_copy(sd[:, bass.ds(g * Q, Q), 0:2 * c.H], src[:, :, D:D + 2 * c.H]).then_inc(s["proj_sd"], 1)
                dve.wait_ge(s["s_row_turned"], g + 1)
                if not isinstance(g, int) or g >= 2:
                    dve.wait_ge(s[f"s_stored{parity}"], 16 * per(g, 2))
                nc.vector.tensor_copy(s_row[0:c.H, parity, :], ps[0:c.H, (6 + parity) * CH:(7 + parity) * CH]
                                      ).then_inc(s["s_row_copied"], 1)

            group(0, 0)
            group(1, 1)
            with dve.Fori(1, NC // 2, 1) as g_at:
                g = g_at * 2
                group(g, 0)
                group(g + 1, 1)
            if L:
                after_projection(NC - 1, 1)

        def layer_dve(dve, L):
            s, c = S[L], Shape(HEADS[L])
            H, dh, w = c.H, c.dh, c.w
            n = NT * H
            dve.wait_ge(s["proj_sd"], NC)
            nc.vector.tensor_reduce(d_max[:, 0:H], sd[:, :, H:2 * H].rearrange("p t h -> p h t"), AX_X, ALU.max
                                    ).then_inc(s["d_max"], 1)
            flat = lambda a: a.rearrange("p (t h) -> p t h", h=H)
            sv, dv = sd[:, :, 0:H], sd[:, :, H:2 * H]
            nc.vector.tensor_scalar(flat(neg_d[:, 0:n]), dv, -1.0, None, ALU.mult).then_inc(s["neg"], 1)
            nc.vector.tensor_scalar(flat(steep_d[:, 0, 0:n]), dv, STEEP, None, ALU.mult).then_inc(s["neg"], 1)
            if c.split:
                nc.vector.tensor_scalar(flat(steep_d[:, 1, 0:n]), dv, -STEEP, None, ALU.mult).then_inc(s["neg"], 1)
            dve.wait_ge(s["d_top"], 1)
            tb = d_top[:, 0:H].unsqueeze(1).to_broadcast([P, NT, H])
            nc.vector.tensor_tensor(flat(d_rel[:, 0:n]), dv, tb, ALU.subtract).then_inc(s["rel"], 1)
            nc.vector.tensor_tensor(flat(s_top[:, 0:n]), sv, tb, ALU.add).then_inc(s["s_top"], 1)
            dve.wait_ge(s["s_top"], 1)
            nc.vector.tensor_scalar(s_lim[:, 0, 0:n], s_top[:, 0:n], 1.0 - SLOPE, 0.0, ALU.mult, ALU.min).then_inc(s["rel"], 1)
            nc.vector.tensor_scalar(s_lim[:, 1, 0:n], s_top[:, 0:n], SLOPE - 1.0, 0.0, ALU.mult, ALU.min).then_inc(s["rel"], 1)

            def product(g, parity):
                pv = prod[:, parity, 0:Q * H * 2 * w].rearrange("p (t h e w) -> p t h e w", t=Q, h=H, e=2)
                efv = ef[:, :, 0:n].rearrange("p e (t h) -> p e t h", h=H)
                if not isinstance(g, int) or g >= 2:
                    dve.wait_ge(s["hi"], g - 1)
                    dve.wait_ge(s["r1"], g - 1)
                nc.vector.tensor_tensor(
                    pv[:, :, :, 0, 0:dh], wh[:, bass.ds(g * Q, Q), :].rearrange("p t (h d) -> p t h d", h=H),
                    efv[:, 0, bass.ds(g * Q, Q), :].unsqueeze(3).to_broadcast([P, Q, H, dh]), ALU.mult).then_inc(s["prod"], 1)

            def parts(g, parity):
                pv, rv = prod_view(prod, parity, c), prod_view(rest, parity, c)
                dve.wait_ge(s["hi"], g + 1)
                if not isinstance(g, int) or g >= 2:
                    dve.wait_ge(s["mid"], g - 1)
                    dve.wait_ge(s["table"], g - 1)
                nc.vector.tensor_tensor(rv, pv, table_view(g, 0, c), ALU.subtract).then_inc(s["r1"], 1)
                dve.wait_ge(s["mid"], g + 1)
                dve.wait_ge(s["r1"], g + 1)
                nc.vector.tensor_tensor(table_view(g, 2, c), rv, table_view(g, 1, c), ALU.subtract).then_inc(s["table"], 1)

            dve.wait_ge(s["ef"], 1)
            dve.wait_ge(s["proj_wh"], NC)
            product(0, 0)
            product(1, 1)
            parts(0, 0)
            parts(1, 1)
            with dve.Fori(1, NC // 2, 1) as g_at:
                g = g_at * 2
                product(g, 0)
                product(g + 1, 1)
                parts(g, 0)
                parts(g + 1, 1)

            dve.wait_ge(s["neg"], 3 if c.split else 2)

            def sweep(row, h, gi, u, sw, mask_at, flip, between):
                for k in range(NT):
                    slot = k % RING
                    if k == REDUCE_AT:
                        between()
                    if k % 2 == 0 and (v_after(sw, 1) or k >= RING):
                        dve.wait_ge(s["step_used"], u + (k + 2 - RING))
                    dst = steps[:, slot, :].rearrange("p (q c) -> p q c", q=Q)
                    mk = run(adjT_b, mask_at + k * P * 2, P, BF16)
                    if k in ON_ACT:
                        i = ON_ACT.index(k)
                        dve.wait_ge(s["gate"], gi + i + 1)
                        nc.vector.tensor_tensor(dst, gates[:, i % GATES, :].rearrange("p (q c) -> p q c", q=Q), mk, ALU.mult
                                                ).then_inc(s["gate_used"], 1)
                    else:
                        at = h + k * H
                        nc.vector.scalar_tensor_tensor(out=dst, in0=row, scalar=neg_d[:, at:at + 1], in1=mk,
                                                       op0=ALU.is_lt if flip else ALU.is_ge, op1=ALU.mult
                                                       ).then_inc(s["step"], 1)

            def reduce(m, parity, hf):
                sw = m * 2 + hf
                dve.wait_ge(s["step_used"], (sw + 1) * NT)
                if v_after(m, 1):
                    dve.wait_ge(x_ready[L], m if c.split else sw - 1)
                if c.split:
                    src = ps[:, hf * 4 * CH:(hf + 1) * 4 * CH].rearrange("p (q c) -> p q c", q=Q)[:, :, 0:3 * w]
                    nc.vector.tensor_reduce(red[:, hf, 0:Q * w].rearrange("p (q w) -> p q w", q=Q),
                                            src.rearrange("p q (s w) -> p q w s", s=3), AX_X, ALU.add).then_inc(s["reduced"], 1)
                    return
                if hf:
                    a0 = (4 + 2 * parity) * CH
                    srca = ps[:, a0:a0 + 2 * CH].rearrange("p (q c) -> p q c", q=Q)[:, :, 0:6 * w]
                    nc.vector.tensor_reduce(red_a[:, 0:Q * 2 * w].rearrange("p (q h w) -> p q h w", q=Q, h=2),
                                            srca.rearrange("p q (h s w) -> p q h w s", h=2, s=3), AX_X, ALU.add)
                src = ps[:, 2 * hf * CH:(2 * hf + 2) * CH].rearrange("p (q c) -> p q c", q=Q)[:, :, 0:6 * w]
                nc.vector.tensor_reduce(red[:, hf, 0:Q * 2 * w].rearrange("p (q e w) -> p q e w", q=Q, e=2),
                                        src.rearrange("p q (e s w) -> p q e w s", e=2, s=3), AX_X, ALU.add).then_inc(s["reduced"], 1)

            def pair(m, parity):
                dve.wait_ge(s["s_bc_in"], 16 * (m + 1))
                dve.wait_ge(s["adjT_in"], 16 * (ig_of(L, m) + 1))
                for hf in range(2):
                    sw = m * 2 + hf
                    if hf:
                        between = lambda: reduce(m, parity, 0)
                    else:
                        between = (lambda: reduce(m - 1, 1 - parity, 1)) if v_after(m, 1) else (lambda: None)
                    sweep(s_row_of(c, parity, hf).rearrange("p (q c) -> p q c", q=Q), head_of(c, parity, hf),
                          held(dve, sw * len(ON_ACT)), held(dve, sw * NT), sw,
                          held(dve, adjT_half(c, m, parity, hf)), c.split and hf, between)

            each_pair(dve, c, pair)
            reduce(NC * c.pairs - 1, 1, 1)

        def elu_pair(dve, g):
            rows = lambda a, n: a[:, bass.ds(n * Q, Q), :].rearrange("p t d -> p (t d)")
            for parity in range(2):
                o, xv = rows(o_all, g + parity), rows(x_sb, g + parity)
                if v_after(g, 2):
                    dve.wait_ge(tail["y"], g)
                nc.vector.tensor_scalar(s_bc[:, parity * CH:(parity + 1) * CH], o, 0.0, None, ALU.min
                                        ).then_inc(tail["neg"], 1)
                nc.vector.scalar_tensor_tensor(out=xv, in0=o, scalar=0.0, in1=xv, op0=ALU.max, op1=ALU.add
                                               ).then_inc(tail["sum"], 1)
            for parity in range(2):
                xv = rows(x_sb, g + parity)
                dve.wait_ge(tail["exp"], g + parity + 1)
                dve.wait_ge(tail["sum"], g + parity + 1)
                nc.vector.scalar_tensor_tensor(out=xv, in0=s_bc[:, parity * CH:(parity + 1) * CH], scalar=-1.0,
                                               in1=xv, op0=ALU.add, op1=ALU.add).then_inc(tail["y"], 1)

        @block.vector
        def _(dve):
            layer_stats(dve, 0)
            dve.wait_ge(w_turned, 1)
            nc.vector.tensor_copy(w_turn[:, :, :].rearrange("p a b -> p (a b)"), ps[:, 6 * CH:6 * CH + 3 * P]).then_inc(w_copied, 1)
            dve.wait_ge(wa_ready, 1)
            for i, L in enumerate(HEADS):
                w = w_turn[:, 0, :] if i == 0 else w_in[:, i, :]
                nc.vector.tensor_copy(w_ext[L][:, 0:D], w).then_inc(w_done, 1)
                nc.vector.tensor_copy(w_ext[L][:, D:D + 2 * HEADS[L]],
                                      ps[:, 7 * CH + 8 * i:7 * CH + 8 * i + 2 * HEADS[L]]).then_inc(w_done, 1)
            layer_norm(dve, 0)

            def cast(t, parity, ch):
                nc.vector.tensor_scalar(mask[:, parity, ch * CH:(ch + 1) * CH], adj_in[:, parity, ch * CH:(ch + 1) * CH],
                                        0.0, -1.0, ALU.is_gt, ALU.add).then_inc(mask_ready, 1)

            def update(v, parity, last=False):
                dve.wait_ge(p_ready, (v + 1) * NC)
                nc.vector.tensor_reduce(den0[:, parity:parity + 1], row_sum[:, parity, :], AX_X, ALU.add).then_inc(row_step, 1)
                done = 3 * v + 2 - last
                dve.wait_ge(row_step, done + 1)
                nc.vector.reciprocal(rden0[:, parity:parity + 1], den0[:, parity:parity + 1]).then_inc(row_step, 1)
                dve.wait_ge(row_step, done + 2)
                dve.wait_ge(prob_used, (v + 1) * NC)
                xv = x_sb[:, bass.ds(v, 1), :].rearrange("p a d -> p (a d)")
                nc.vector.scalar_tensor_tensor(out=xv, in0=ps[:, 7 * CH:7 * CH + D],
                                               scalar=rden0[:, parity:parity + 1], in1=xv,
                                               op0=ALU.mult, op1=ALU.add).then_inc(x_ready[0], 1)

            def step(t, parity, scores=True, probs=True, upd=True, nxt=True):
                v = t - 1
                first = isinstance(t, int)
                for ch in range(NC + LAG):
                    if nxt and ch < NC:
                        if ch == 0:
                            dve.wait_ge(adj_loaded[1 - parity], 16 * (per(t + 1, 2) + 1))
                        if not first or t >= 1:
                            dve.wait_ge(mt_turned, (t - 1) * NC + ch + 1)
                        if scores:
                            if ch == 0 and (not first or t >= 2):
                                dve.wait_ge(turned, (t - 1) * NC)
                            dve.wait_ge(relu_ready, t * NC + ch + 1)
                        cast(t + 1, 1 - parity, ch)
                    if scores and ch < NC:
                        if not nxt:
                            if ch == 0:
                                dve.wait_ge(turned, (t - 1) * NC)
                            dve.wait_ge(relu_ready, t * NC + ch + 1)
                        nc.vector.tensor_tensor_reduce(
                            out=score[:, parity, ch * CH:(ch + 1) * CH], in0=ps[:, (ch % 4) * CH:(ch % 4 + 1) * CH],
                            in1=relu4[:, ch % 4, :], scale=SLOPE, scalar=-3e38, op0=ALU.add, op1=ALU.max,
                            accum_out=row_max[:, parity, ch:ch + 1]).then_inc(score_ready, 1)
                    if probs and ch >= LAG:
                        cc = ch - LAG
                        nv = v * NC + cc
                        dve.wait_ge(turned, nv + 1)
                        if not first or nv >= 4:
                            dve.wait_ge(prob_used, nv - 3)
                        nc.vector.tensor_copy(prob_T[:, cc % 4, :], ps[:, (5 + cc % 2) * CH:(6 + cc % 2) * CH]).then_inc(prob_ready, 1)
                    if ch == 1 and upd:
                        update(t - 2, parity)
                if scores:
                    dve.wait_ge(score_ready, (t + 1) * NC)
                    if not first or t >= 2:
                        dve.wait_ge(p_ready, (t - 1) * NC)
                    nc.vector.tensor_reduce(row_top[:, parity:parity + 1], row_max[:, parity, :], AX_X, ALU.max).then_inc(row_step, 1)
                    dve.wait_ge(row_step, top_count(t))
                    nc.vector.tensor_scalar(neg_max[:, parity:parity + 1], row_top[:, parity:parity + 1], -1.0, None,
                                            ALU.mult).then_inc(neg_ready, 1)

            def top_count(t):
                return t + 1 if isinstance(t, int) and t < 2 else 3 * t - 1

            dve.wait_ge(adj_loaded[0], 16)
            for ch in range(NC):
                cast(0, 0, ch)
            step(0, 0, probs=False, upd=False)
            step(1, 1, upd=False)
            with dve.Fori(1, NT // 2 - 1, 1) as t_at:
                t = t_at * 2
                step(t, 0)
                step(t + 1, 1)
            step(NT - 2, 0)
            step(NT - 1, 1, nxt=False)
            step(NT, 0, scores=False, nxt=False)
            update(NT - 1, 1, last=True)

            for L in HEADS:
                if L >= layers:
                    break
                layer_stats(dve, L)
                layer_norm(dve, L)
                layer_dve(dve, L)
            if layers == 4:
                dve.wait_ge(x_ready[3], X_DONE[3])
                elu_pair(dve, 0)
                with dve.Fori(1, NC // 2, 1) as g_at:
                    elu_pair(dve, g_at * 2)

        def h_turn(pe, L):
            s = S[L]
            buf = norm0 if L == 0 else norm

            def group(g, parity):
                pe.wait_ge(s["normed"], (g + 1) * Q)
                if not isinstance(g, int) or g >= 2:
                    pe.wait_ge(s["h_done"], g - 1)
                for q in range(Q):
                    last = nc.tensor.transpose(ps[:, parity * CH + q * P:parity * CH + (q + 1) * P],
                                               buf[:, parity, q, :], ident[:, :])
                last.then_inc(s["h_turned"], 1)
                if L:
                    c = Shape(HEADS[L])
                    pe.wait_ge(s["h_done"], g + 1)
                    if not isinstance(g, int) or g >= 2:
                        pe.wait_ge(s["proj_wh"], g - 1)
                        pe.wait_ge(s["s_row_copied"], g - 1)
                    nc.tensor.matmul(ps[0:c.H, (6 + parity) * CH:(7 + parity) * CH], w_ext[L][:, D:D + c.H],
                                     h_grp[:, parity, :], start=True, stop=True).then_inc(s["s_row_turned"], 1)
                    for q in range(Q):
                        at = (2 + 2 * parity) * CH + q * 2 * P
                        last = nc.tensor.matmul(ps[:, at:at + D + 2 * c.H], h_grp[:, parity, q * P:(q + 1) * P],
                                                w_ext[L][:, :], start=True, stop=True, skip_group_check=True)
                    last.then_inc(s["proj"], 1)

            group(0, 0)
            group(1, 1)
            with pe.Fori(1, NC // 2, 1) as g_at:
                g = g_at * 2
                group(g, 0)
                group(g + 1, 1)

        def layer_pe(pe, L):
            s, c = S[L], Shape(HEADS[L])
            w = c.w
            pe.wait_ge(s["table"], NC)
            pe.wait_ge(s["proj_sd"], NC)

            def sweep(head, gi, ni, mask_at, parity, hf):
                for k in range(NT):
                    slot = k % RING
                    if k in ON_ACT:
                        pe.wait_ge(s["gate_used"], gi + ON_ACT.index(k) + 1)
                    else:
                        pe.wait_ge(s["step"], ni + ALONE.index(k) + 1)
                    start = k == 0
                    tab = k * TROW + head * 6 * w
                    if c.split:
                        rows = table[:, tab + hf * 3 * w:tab + (hf + 1) * 3 * w]
                        for q in range(Q):
                            at = (hf * 4 + q) * CH
                            last = nc.tensor.matmul(ps[:, at:at + 3 * w], steps[:, slot, q * P:(q + 1) * P], rows,
                                                    start=start, stop=False, skip_group_check=True)
                    else:
                        rows = table[:, tab:tab + 6 * w]
                        by_mask = k % 2 == hf
                        both = table[:, tab - hf * 6 * w:tab + (2 - hf) * 6 * w].rearrange("p (h e c) -> p h e c", h=2, e=2)
                        for q in range(Q):
                            at = 2 * hf * CH + q * 2 * P
                            last = nc.tensor.matmul(ps[:, at:at + 6 * w], steps[:, slot, q * P:(q + 1) * P], rows,
                                                    start=start and q % 2 == 0, stop=False, skip_group_check=True)
                            if by_mask:
                                at = (4 + 2 * parity) * CH + q * 2 * P
                                mk = run(adjT_b[:, q], mask_at + k * P * 2, P, BF16)
                                last = nc.tensor.matmul(ps[:, at:at + 6 * w], mk, both[:, :, 1, :],
                                                        start=start and q % 2 == 0, stop=False, skip_group_check=True)
                    last.then_inc(s["step_used"], 1)

            def pair(m, parity):
                pe.wait_ge(s["adjT_in"], 16 * (ig_of(L, m) + 1))
                for hf in range(2):
                    sw = m * 2 + hf
                    if v_after(sw, 2):
                        pe.wait_ge(s["reduced"], sw - 1)
                    sweep(head_of(c, parity, hf), held(pe, sw * len(ON_ACT)), held(pe, sw * len(ALONE)),
                          held(pe, adjT_half(c, m, parity, hf)), parity, hf)

            each_pair(pe, c, pair)

        @block.tensor
        def _(pe):
            pe.wait_ge(set_up, 8)
            pe.wait_ge(loaded["ks"], 16)
            for g in range(NC):
                if g >= 2:
                    pe.wait_ge(ks_copied, g - 1)
                for q in range(Q):
                    last = nc.tensor.transpose(ps[:, (g % 2) * CH + q * P:(g % 2) * CH + (q + 1) * P],
                                               ks_nat[:, g * Q + q, :], ident[:, :])
                last.then_inc(ks_turned, 1)
            pe.wait_ge(loaded["w"], 48)
            for i in range(3):
                last = nc.tensor.transpose(ps[:, 6 * CH + i * P:6 * CH + (i + 1) * P], w_in[:, i, :], ident[:, :])
            last.then_inc(w_turned, 1)
            pe.wait_ge(w_copied, 1)
            pe.wait_ge(loaded["a"], 16 * 18)
            for i in range(3):
                w = w_in[:, 0, :] if i == 0 else w_turn[:, i, :]
                last = nc.tensor.matmul(ps[:, 7 * CH + 8 * i:7 * CH + 8 * i + 8], w, a_blk[:, i, :], start=True, stop=True,
                                        skip_group_check=True)
            last.then_inc(wa_ready, 1)
            pe.wait_ge(ks_copied, NC)
            h_turn(pe, 0)
            pe.wait_ge(S[0]["h_done"], NC)
            pe.wait_ge(w_done, 6)

            def step(t, parity, scores=True, probs=True):
                v, vp = t - 1, 1 - parity
                first = isinstance(t, int)
                for ch in range(NC + LAG + 1):
                    if scores and ch < NC:
                        n = t * NC + ch
                        if ch == 0:
                            pe.wait_ge(h_tile_ready, t + 1)
                        if not first or n >= 4:
                            pe.wait_ge(score_ready, n - 3)
                        pe.wait_ge(mask_ready, n + 1)
                        bank = ps[:, (ch % 4) * CH:(ch % 4 + 1) * CH]
                        nc.tensor.matmul(bank, h_tile[:, parity, :], ks_T[:, ch * CH:(ch + 1) * CH], start=True, stop=False)
                        nc.tensor.matmul(bank, big_ident[:, :], mask[:, parity, ch * CH:(ch + 1) * CH],
                                         start=False, stop=True).then_inc(s_ready, 1)
                        if not first or n >= 1:
                            pe.wait_ge(mt_copied, n)
                        for q in range(Q):
                            at = 4 * 2 * CH + q * P
                            last = nc.tensor.transpose(ps_b[:, at:at + P],
                                                       mask[:, parity, ch * CH + q * P:ch * CH + (q + 1) * P], identb[:, :])
                        last.then_inc(mt_turned, 1)
                    if probs and LAG <= ch < NC + LAG:
                        cc = ch - LAG
                        nv = v * NC + cc
                        pe.wait_ge(p_ready, nv + 1)
                        if not first or nv >= 2:
                            pe.wait_ge(prob_ready, nv - 1)
                        for q in range(Q):
                            at = (5 + cc % 2) * CH + q * P
                            last = nc.tensor.transpose(ps[:, at:at + P],
                                                       score[:, vp, cc * CH + q * P:cc * CH + (q + 1) * P], ident[:, :])
                        last.then_inc(turned, 1)
                    if probs and ch > LAG:
                        cc = ch - LAG - 1
                        nv = v * NC + cc
                        pe.wait_ge(prob_ready, nv + 1)
                        if cc == 0 and (not first or v >= 1):
                            pe.wait_ge(x_ready[0], v)
                        for q in range(Q):
                            last = nc.tensor.matmul(ps[:, 7 * CH:7 * CH + D],
                                                    prob_T[:, cc % 4, q * P:(q + 1) * P], ks_nat[:, cc * Q + q, :],
                                                    start=(cc == 0 and q == 0), stop=(cc == NC - 1 and q == Q - 1),
                                                    skip_group_check=True)
                        last.then_inc(prob_used, 1)

            step(0, 0, probs=False)
            step(1, 1)
            with pe.Fori(1, NT // 2, 1) as t_at:
                t = t_at * 2
                step(t, 0)
                step(t + 1, 1)
            step(NT, 0, scores=False)

            for L in HEADS:
                if L >= layers:
                    break
                pe.wait_ge(x_ready[L - 1], X_DONE[L - 1])
                h_turn(pe, L)
                layer_pe(pe, L)


_INS = ["x", "adj", "L0_gnn_ks", "L1_gnn_W", "L1_gnn_attn_src", "L1_gnn_attn_dst", "L2_gnn_W", "L2_gnn_a",
        "L3_gnn_W", "L3_gnn_a"]
LAYERS = 4


def kernel(**inputs):
    import numpy as _np
    import concourse.bacc as _bacc
    from concourse import mybir as _mybir
    from concourse.bass_utils import run_bass_kernel_spmd as _run

    nc = _bacc.Bacc("TRN2", target_bir_lowering=False, num_devices=1)
    arrays, args = {}, []
    for name in _INS:
        a = _np.ascontiguousarray(inputs[name])
        arrays[f"in_{name}_dram"] = a
        args.append(nc.dram_tensor(f"in_{name}_dram", a.shape, _mybir.dt.from_np(a.dtype), kind="ExternalInput").ap())
    args.append(nc.dram_tensor("out_0_dram", (N, D), F32, kind="ExternalOutput").ap())
    bass_gnn_stack_kernel(nc, *args, layers=LAYERS)
    r = _run(nc, [arrays], core_ids=[0])
    return r.results[0]["out_0_dram"]
```

```python
from contextlib import ExitStack

import concourse.bass as bass
from concourse import mybir

F32 = mybir.dt.float32
BF16 = mybir.dt.bfloat16
I32 = mybir.dt.int32
U8 = mybir.dt.uint8
BYTES = {F32: 4, I32: 4, BF16: 2, U8: 1}
ALU = mybir.AluOpType
ACT = mybir.ActivationFunctionType
AX_X = mybir.AxisListType.X
RMAX = bass.bass_isa.ReduceOp.max

N, D, P = 4096, 128, 128
NT = N // P
CH = 512
NC = N // CH
Q = CH // P
EPS = 1e-5
SLOPE = 0.2
BIG = 2.0 ** 100
STEEP = 2.0 ** 50
RING = 8
ON_ACT = [k for k in range(NT) if k % 16 not in (2, 5, 8, 11, 14)]
ALONE = [k for k in range(NT) if k not in ON_ACT]
GATES = len(ON_ACT) // 2
REDUCE_AT = 10
STATS_AT = 26
STAT_TILES = 8
PRODS = 3
RESTS = 3
A_LOADS = 4 * 4 + 2
PIECES = 4
LAG = 2

HEADS = {1: 4, 2: 1, 3: 4}


def live(t):
    return not isinstance(t, int) or 0 <= t < NT


def lagging(t, ch, lag):
    return (t - 1, ch - lag) if ch >= lag else (t - 2, ch - lag + NC)


def due(a, least):
    return not isinstance(a, int) or a >= least


def held(eng, a):
    return a if isinstance(a, int) else eng.snap(a)


def odd(a):
    return a % 2 if isinstance(a, int) else a & 1


class Shape:

    def __init__(self, heads):
        self.H = heads
        self.dh = D // heads
        self.w = self.dh + 1
        self.row = heads * 2 * 3 * self.w
        self.pairs = 2 if heads > 1 else 1
        self.split = heads == 1


def bass_gnn_stack_kernel(nc, x, adj, ks, w1, a1_src, a1_dst, w2, a2, w3, a3, out):
    ctx = ExitStack()
    with ctx:
        top = [(nc.sbuf_base + 31) // 32 * 32]

        def place(name, shape, dtype, at=None):
            size = 1
            for n in shape[1:]:
                size *= n
            size *= BYTES[dtype]
            if at is None:
                at = top[0]
                top[0] = (at + size + 31) // 32 * 32
            return nc.alloc_sbuf_tensor_at(name, shape, dtype, offset=at)

        def place_bytes(name, shape, dtype):
            b = place(name, shape[:-1] + [shape[-1] * BYTES[dtype]], U8)
            return b, b[(slice(None),) * len(shape)].bitcast(dtype)

        def run(view, at, n, dtype):
            return view[(slice(None),) * (len(view.shape) - 1) + (bass.ds(at, n * BYTES[dtype]),)].bitcast(dtype)

        def sem(name):
            return ctx.enter_context(nc.semaphore(name))

        x_sb = place("x_sb", [P, NT, D], F32)
        ident = place("ident", [P, P], F32)
        identb = place("identb", [P, P], BF16)
        big_ident = place("big_ident", [P, P], BF16)
        ones_col = place("ones_col", [P, 1], F32)
        minus_half = place("minus_half", [P, STAT_TILES], F32)
        minus_one = place("minus_one", [P, 2 * Q], F32)
        w_ext = {L: place(f"w_ext{L}", [P, D + 2 * HEADS[L]], F32) for L in HEADS}
        warm = place("warm", [P, 2 * len(HEADS)], F32)
        stats = place("stats", [P, NT, 6], F32)
        mean = place("mean", [P, NT], F32)
        rstd = place("rstd", [P, NT], F32)
        st_tmp = place("st_tmp", [P, 7, STAT_TILES], F32)
        stat_const = place("stat_const", [P, 3, STAT_TILES], F32)
        phase = top[0]

        ks_T = place("ks_T", [P, N], F32)
        ks_nat = place("ks_nat", [P, NT, D], F32)
        adj_in = place("adj_in", [P, 2, N], I32)
        mask = place("mask", [P, 2, N], BF16)
        relu4 = place("relu4", [P, 4, CH], F32)
        score = place("score", [P, 2, N], F32)
        prob_T = place("prob_T", [P, 4, CH], F32)
        adjT_out = place("adjT_out", [P, 2, NT, P], BF16)
        h_T = place("h_T", [P, N], F32)
        h_tile = place("h_tile", [P, 2, P], F32)
        norm0 = place("norm0", [P, 2, Q, D], F32)
        row_max = place("row_max", [P, 2, NC], F32)
        row_top = place("row_top", [P, 2], F32)
        neg_max = place("neg_max", [P, 2], F32)
        row_sum = place("row_sum", [P, 2, NC], F32)
        den0 = place("den0", [P, 2], F32)
        rden0 = place("rden0", [P, 2], F32)
        w_in = place("w_in", [P, 3, P], F32)
        w_turn = place("w_turn", [P, 3, P], F32)
        a_blk = place("a_blk", [P, 3, 8], F32)

        top[0] = phase
        TROW = max(Shape(h).row for h in HEADS.values())
        WMAX = max(Shape(h).w for h in HEADS.values())
        SUMS_W = Shape(4).w
        PROD = Q * max(HEADS.values()) * 2 * SUMS_W
        table = place("table", [P, NT * TROW], BF16)
        adjT_b, adjT = place_bytes("adjT", [P, Q, 2 * NT * P], BF16)
        s_bc = place("s_bc", [P, 4 * CH], F32)
        at = top[0]
        norm = place("norm", [P, 2, Q, D], F32)
        h_grp = place("h_grp", [P, 2, CH], F32)
        after = top[0]
        top[0] = at
        steps = place("steps", [P, RING, CH], BF16)
        gates = place("gates", [P, GATES, CH], BF16)
        third_prod = place("third_prod", [P, 1, PROD], F32, at=at)
        top[0] = max(top[0], after)
        at = top[0]
        prod = place("prod", [P, 2, PROD], F32)
        third = top[0] + (RESTS - 1) * PROD * 4
        rest = place("rest", [P, RESTS, PROD], F32)
        s_lim = place("s_lim", [P, 2, NT * 4], F32, at=third)
        s_top = place("s_top", [P, NT * 4], F32, at=third + 2 * NT * 4 * 4)
        after = top[0]
        top[0] = at
        red = place("red", [P, 2, 2 * Q * WMAX], F32)
        red_a = place("red_a", [P, 2 * Q * SUMS_W], F32)
        pt = [place(f"pt{i}", [P, Q * WMAX], F32) for i in range(3)]
        assert top[0] <= after
        top[0] = after
        at = top[0]
        wh = place("wh", [P, NT, D + 4], F32)
        o_all = place("o_all", [P, NT, D], F32, at=at)
        s_row = place("s_row", [P, P], F32)
        sd = place("sd", [P, 2, NT * 4], F32)
        d_max = place("d_max", [P, 4], F32)
        d_top = place("d_top", [P, 4], F32)
        d_rel = place("d_rel", [P, NT * 4], F32)
        ef = place("ef", [P, 2, NT * 4], F32)
        ab = place("ab", [P, 2, NT * 4], F32)
        neg_d = place("neg_d", [P, NT * 4], F32)
        steep_d = place("steep_d", [P, 2, NT * 4], F32)
        rden = place("rden", [P, 2 * Q], F32)
        assert top[0] <= nc.sbuf_usable_end, (top[0], nc.sbuf_usable_end)

        ps = ctx.enter_context(nc.psum_tensor("ps", [P, 8 * CH], F32))
        ps_b = ps[:, :].bitcast(BF16)

        adjT_d = nc.dram_tensor("adjT_d", [NT, P, NT * P], BF16).ap()
        s_d = {L: nc.dram_tensor(f"s_d{L}", [HEADS[L], N], F32).ap() for L in HEADS}

        loaded = {n: sem(f"loaded_{n}") for n in ("w", "a")}
        x_loaded = [sem(f"x_loaded{i}") for i in range(PIECES)]
        ks_loaded = [sem(f"ks_loaded{i}") for i in range(PIECES)]
        set_up = sem("set_up")
        w_turned = sem("w_turned")
        w_copied = sem("w_copied")
        wa_ready = sem("wa_ready")
        w_done = sem("w_done")
        ks_turned = sem("ks_turned")
        ks_copied = sem("ks_copied")
        adj_loaded = [sem("adj_loaded0"), sem("adj_loaded1")]
        mask_ready = sem("mask_ready")
        h_tile_ready = sem("h_tile_ready")
        s_ready = sem("s_ready")
        relu_ready = sem("relu_ready")
        score_ready = sem("score_ready")
        neg_ready = sem("neg_ready")
        p_ready = sem("p_ready")
        turned = sem("turned")
        prob_ready = sem("prob_ready")
        prob_used = sem("prob_used")
        mt_turned = sem("mt_turned")
        mt_copied = sem("mt_copied")
        adjT_stored = [sem("adjT_stored0"), sem("adjT_stored1")]
        x_ready = {L: sem(f"x_ready{L}") for L in range(4)}
        row_step = sem("row_step")
        stored = sem("stored")

        block = ctx.enter_context(nc.Block())

        ig_of = lambda L, m: m // Shape(HEADS[L]).pairs
        S = {}
        for L in [0] + list(HEADS):
            names = ["stat", "stat_step", "normed", "h_turned", "h_done"]
            if L:
                names += ["proj", "proj_wh", "proj_sd", "s_row_turned", "s_row_copied", "d_max", "d_top", "s_top",
                          "rel", "ef", "neg", "prod", "ones", "hi", "r1", "mid", "table", "s_stored",
                          "adjT_in", "s_bc_in", "gate", "gate_used", "step", "step_used", "reduced", "pool_step"]
            S[L] = {n: sem(f"L{L}_{n}") for n in names}
        tail = {n: sem(f"tail_{n}") for n in ("neg", "exp", "sum", "y")}
        X_DONE = {0: NT, **{L: NC * Shape(h).pairs for L, h in HEADS.items()}}

        def layer0_stored(eng):
            for done in adjT_stored:
                eng.wait_ge(done, 16 * NT // 2)

        def group_rows(a, g):
            return a[:, bass.ds(g * Q, Q), :].rearrange("p t d -> p (t d)")

        def head_of(c, parity, hf):
            return 0 if c.split else parity * 2 + hf

        def s_row_of(c, parity, hf):
            slot = parity if c.split else parity * 2 + hf
            return s_bc[:, slot * CH:(slot + 1) * CH]

        def table_view(g, part, c):
            t = table[:, :].rearrange("p (t r) -> p t r", t=NT)[:, bass.ds(g * Q, Q), 0:c.row]
            return t.rearrange("p t (b s w) -> p t b s w", s=3, w=c.w)[:, :, :, part, :]

        def wh_view(t, n, c):
            return wh[:, bass.ds(t, n), 0:c.H * c.w].rearrange("p t (h w) -> p t h w", h=c.H)

        def prod_slot(g, c):
            return prod_view(third_prod, 0, c) if g % PRODS == 2 else prod_view(prod, g % PRODS, c)

        def prod_view(b, parity, c):
            return b[:, parity, 0:Q * c.H * 2 * c.w].rearrange("p (t b w) -> p t b w", t=Q, w=c.w)

        def adjT_half(c, m, parity, hf):
            if c.split:
                return parity * (NT * P * 2)
            return m // 2 % 2 * (NT * P * 2) if hf else (m & 2) * (NT * P)

        def each_pair(eng, c, pair):
            last = NC * c.pairs - 1
            pair(0, 0)
            with eng.Fori(1, NC * c.pairs // 2, 1) as at:
                pair(at * 2 - 1, 1)
                pair(at * 2, 0)
            pair(last, 1)

        def layer_dma(sp, L):
            s, c = S[L], Shape(HEADS[L])

            def load_adjT(ig, parity):
                sp.dma_start(adjT[:, :, parity * NT * P:(parity + 1) * NT * P],
                             adjT_d[bass.ds(ig * Q, Q)].rearrange("q p c -> p q c")).then_inc(s["adjT_in"], 16)

            def load_s(m):
                ig = ig_of(L, m)
                if c.split:
                    rows, slot, n = 0, odd(m), 1
                else:
                    rows, slot, n = odd(m) * 2, odd(m) * 2, 2
                src = s_d[L][bass.ds(rows, n), bass.ds(ig * CH, CH)]
                sp.dma_start(s_bc[:, bass.ds(slot * CH, n * CH)].rearrange("p (h c) -> p h c", h=n),
                             src.partition_broadcast(P)).then_inc(s["s_bc_in"], 16)

            sp.wait_ge(x_ready[L - 1], X_DONE[L - 1])
            sp.wait_ge(s["s_row_copied"], 1)
            sp.dma_start(s_d[L].rearrange("h (t r) -> (h t) r", r=P), s_row[0:NT * c.H, :]).then_inc(s["s_stored"], 16)
            sp.wait_ge(s["s_stored"], 16)
            load_s(0)
            sp.wait_ge(s["s_bc_in"], 16)
            load_s(1)
            load_adjT(0, 0)
            sp.wait_ge(s["table"], NC)
            sp.wait_ge(s["adjT_in"], 16)
            load_adjT(1, 1)

            def next_s(m):
                sp.wait_ge(s["gate_used"], 2 * (m + 1) * len(ON_ACT))
                sp.wait_ge(s["s_bc_in"], 16 * (m + 2))
                load_s(m + 2)

            with sp.Fori(0, NC // 2 - 1, 1) as ig_at:
                for parity in range(2):
                    ig = ig_at * 2 + parity
                    for pp in range(c.pairs):
                        next_s(ig * c.pairs + pp)
                    sp.wait_ge(s["step_used"], (ig + 1) * 2 * c.pairs * NT)
                    sp.wait_ge(s["adjT_in"], 16 * (ig + 2))
                    load_adjT(ig + 2, parity)
            for m in range((NC - 2) * c.pairs, NC * c.pairs - 2):
                next_s(m)

        @block.sync
        def _(sp):
            for dst, src, done in ((x_sb, x, x_loaded), (ks_nat, ks, ks_loaded)):
                for i in range(PIECES):
                    part = slice(i * NT // PIECES, (i + 1) * NT // PIECES)
                    sp.dma_start(dst[:, part, :], src.rearrange("(t p) d -> p t d", p=P)[:, part, :]).then_inc(done[i], 16)

            def load_adj(t, parity):
                sp.dma_start(adj_in[:, parity, :], adj_tiles(t)).then_inc(adj_loaded[parity], 16)

            def adj_tiles(t):
                return adj[bass.ds(t * P, P), :]

            load_adj(0, 0)
            for i, w in enumerate((w1, w2, w3)):
                sp.dma_start(w_in[:, i, :], w).then_inc(loaded["w"], 16)
            sp.wait_ge(set_up, 5)
            n = 0
            for h in range(4):
                rows = slice(32 * h, 32 * h + 32)
                for src, i, col in ((a1_src[0, h], 0, h), (a1_dst[0, h], 0, 4 + h),
                                    (a3[0, h, 0:32], 2, h), (a3[0, h, 32:64], 2, 4 + h)):
                    sp.dma_start(a_blk[rows, i, col:col + 1], src.unsqueeze(1)).then_inc(loaded["a"], 16)
                    n += 1
            for k in range(2):
                sp.dma_start(a_blk[:, 1, k:k + 1], a2[k * D:(k + 1) * D, :]).then_inc(loaded["a"], 16)
                n += 1
            assert n == A_LOADS
            load_adj(1, 1)

            def step(t, parity, more=True):
                if more:
                    sp.wait_ge(mask_ready, (t + 1) * NC)
                    load_adj(t + 2, parity)
                sp.wait_ge(mt_copied, (t + 1) * NC)
                sp.dma_start(adjT_d[bass.ds(t, 1)].rearrange("a p c -> (a p) c"),
                             adjT_out[:, parity].rearrange("p t c -> p (t c)")).then_inc(adjT_stored[parity], 16)

            with sp.Fori(0, NT // 2 - 1, 1) as t_at:
                t = t_at * 2
                step(t, 0)
                step(t + 1, 1)
            step(NT - 2, 0, more=False)
            step(NT - 1, 1, more=False)
            layer0_stored(sp)

            for L in HEADS:
                layer_dma(sp, L)
            with sp.Fori(0, NC, 1) as g:
                sp.wait_ge(tail["y"], g + 1)
                sp.dma_start(out[bass.ds(g * CH, CH), :].rearrange("(t p) d -> p t d", p=P),
                             x_sb[:, bass.ds(g * Q, Q), :]).then_inc(stored, 16)
            sp.wait_ge(stored, 16 * NC)

        STATS = 10

        def row_stats(pool, L, i, t, n):
            s = S[L]
            k = [0]

            def step(ins):
                k[0] += 1
                ins.then_inc(s["stat_step"], 1)

            def wait():
                pool.wait_ge(s["stat_step"], i * STATS + k[0])

            at = bass.ds(t, n)
            pool.wait_ge(s["stat"], t + n)
            me, mo, ve, vo = (stats[:, at, j] for j in (1, 4, 2, 5))
            t0, t1, t2, t3, t4, t5, veps = (st_tmp[:, j, 0:n] for j in range(7))
            half, per_d, eps = (stat_const[:, j, 0:n] for j in range(3))
            tt = nc.gpsimd.tensor_tensor
            step(tt(t0, me, mo, ALU.add))
            step(tt(t1, me, mo, ALU.subtract))
            step(tt(t2, ve, vo, ALU.add))
            wait()
            step(tt(mean[:, at], t0, half, ALU.mult))
            step(tt(t3, t1, half, ALU.mult))
            step(tt(t4, t2, per_d, ALU.mult))
            wait()
            step(tt(t3, t3, t3, ALU.mult))
            step(tt(t5, t4, eps, ALU.add))
            wait()
            step(tt(veps, t3, t5, ALU.add))
            wait()
            step(tt(rstd[:, at], veps, minus_half[:, 0:n], ALU.pow))

        def layer_pool(pool, L):
            s, c = S[L], Shape(HEADS[L])
            H, dh, w = c.H, c.dh, c.w
            if L == 1:
                layer0_stored(pool)
            nc.gpsimd.memset(wh_view(0, NT, c)[:, :, :, dh], 1.0).then_inc(s["ones"], 1)
            pool.wait_ge(s["d_max"], 1)
            nc.gpsimd.partition_all_reduce(d_top[:, 0:H], d_max[:, 0:H], P, RMAX).then_inc(s["d_top"], 1)

            def last_part(g, slot):
                pool.wait_ge(s["mid"], g + 1)
                nc.gpsimd.tensor_tensor(table_view(g, 2, c), prod_view(rest, slot, c), table_view(g, 1, c),
                                        ALU.subtract).then_inc(s["table"], 1)

            for g in range(NC):
                last_part(g, g % RESTS)

            nh = 1 if c.split else 2
            view = lambda a: a[:, 0:Q * nh * w].rearrange("p (q h w) -> p q h w", q=Q, h=nh)
            ta, tb, tc = (view(a) for a in pt)
            if c.split:
                e_sum, f_sum = (view(red[:, e, :]) for e in range(2))
            else:
                rv = red[:, :, 0:Q * 2 * w].rearrange("p h (q e w) -> p q h e w", q=Q, e=2)
                e_sum, f_sum, a_sum = rv[:, :, :, 0, :], rv[:, :, :, 1, :], view(red_a)
            abv = ab[:, :, 0:NT * H].rearrange("p e (t h) -> p e t h", h=H)
            rd = rden[:, 0:Q * nh].rearrange("p (q h) -> p q h", q=Q)
            STEPS = (4 if c.split else 5) + (L != 3)

            def combine(m, ig, h):
                k = [0]

                def wait():
                    pool.wait_ge(s["pool_step"], m * STEPS + k[0])

                def step(ins):
                    k[0] += 1
                    ins.then_inc(s["pool_step"], 1)

                def factor(e):
                    return abv[:, e, bass.ds(ig * Q, Q), bass.ds(h, nh)].unsqueeze(3).to_broadcast([P, Q, nh, w])

                tt = nc.gpsimd.tensor_tensor
                pool.wait_ge(s["reduced"], 2 * (m + 1))
                fs = f_sum
                if not c.split:
                    step(tt(tb, a_sum, f_sum, ALU.subtract))
                    wait()
                    fs = tb
                step(tt(tc, fs, factor(1), ALU.mult))
                step(tt(ta, e_sum, factor(0), ALU.mult))
                wait()
                step(tt(tb, ta, tc, ALU.add))
                wait()
                step(tt(rd, tb[:, :, :, dh], minus_one[:, 0:Q * nh].rearrange("p (q h) -> p q h", q=Q), ALU.pow))
                wait()
                rb = rd.unsqueeze(3).to_broadcast([P, Q, nh, dh])
                cols = bass.ds(h * dh, nh * dh)
                if L == 3:
                    dst = o_all[:, bass.ds(ig * Q, Q), cols].rearrange("p q (h d) -> p q h d", h=nh)
                    tt(dst, tb[:, :, :, 0:dh], rb, ALU.mult).then_inc(x_ready[L], 1)
                else:
                    step(tt(ta[:, :, :, 0:dh], tb[:, :, :, 0:dh], rb, ALU.mult))
                    wait()
                    xv = x_sb[:, bass.ds(ig * Q, Q), cols].rearrange("p q (h d) -> p q h d", h=nh)
                    tt(xv, xv, ta[:, :, :, 0:dh], ALU.add).then_inc(x_ready[L], 1)
                pool.wait_ge(x_ready[L], m + 1)
                assert k[0] == STEPS

            with pool.Fori(0, NC, 1) as ig:
                for p in range(c.pairs):
                    combine(ig * c.pairs + p, ig, p * 2)
                if L < 3:
                    row_stats(pool, L + 1, ig, ig * Q, Q)

        @block.gpsimd
        def _(pool):
            nc.gpsimd.memset(ident[:, :], 0.0).then_inc(set_up, 1)
            nc.gpsimd.memset(ones_col[:, :], 1.0).then_inc(set_up, 1)
            nc.gpsimd.memset(minus_half[:, :], -0.5).then_inc(set_up, 1)
            nc.gpsimd.memset(a_blk[:, :, :], 0.0).then_inc(set_up, 1)
            nc.gpsimd.memset(minus_one[:, :], -1.0).then_inc(set_up, 1)
            for j, value in enumerate((0.5, 1.0 / D, EPS)):
                nc.gpsimd.memset(stat_const[:, j, :], value).then_inc(set_up, 1)
            pool.wait_ge(set_up, 8)
            nc.gpsimd.affine_select(out=ident[:, :], in_=ident[:, :], compare_op=ALU.not_equal, fill=1.0,
                                    base=0, pattern=[[-1, P]], channel_multiplier=1).then_inc(set_up, 1)
            pool.wait_ge(set_up, 9)
            nc.gpsimd.tensor_copy(identb[:, :], ident[:, :]).then_inc(set_up, 1)
            nc.gpsimd.tensor_scalar(big_ident[:, :], ident[:, :], BIG, 0.0, ALU.mult, ALU.add).then_inc(set_up, 1)

            for i in range(NT // STAT_TILES):
                row_stats(pool, 0, i, i * STAT_TILES, STAT_TILES)

            def step(t, parity):
                pool.wait_ge(s_ready, t * NC)
                nc.gpsimd.tensor_copy(h_tile[:, 1 - parity, :], h_T[:, bass.ds((t + 1) * P, P)]
                                      ).then_inc(h_tile_ready, 1)
                if due(t, 2):
                    row_stats(pool, 1, t - 2, t - 2, 1)

            pool.wait_ge(S[0]["h_done"], NC)
            nc.gpsimd.tensor_copy(h_tile[:, 0, :], h_T[:, 0:P]).then_inc(h_tile_ready, 1)
            for t in range(3):
                step(t, t % 2)
            with pool.Fori(1, NT // 2 - 1, 1) as t_at:
                t = t_at * 2 + 1
                step(t, 1)
                step(t + 1, 0)
            for t in range(NT - 3, NT):
                row_stats(pool, 1, t, t, 1)

            for L in HEADS:
                layer_pool(pool, L)

        def h_relu(act, L):
            s = S[L]
            if L == 1:
                layer0_stored(act)

            def group(g, parity):
                act.wait_ge(s["h_turned"], g + 1)
                if L == 0:
                    dst = h_T[:, bass.ds(g * CH, CH)]
                else:
                    dst = h_grp[:, parity, :]
                    if due(g, 2):
                        act.wait_ge(s["proj"], g - 1)
                nc.scalar.activation(dst, ps[:, parity * CH:(parity + 1) * CH], ACT.Relu).then_inc(s["h_done"], 1)
                if L and due(g, 1):
                    copy_wh(g - 1, 1 - parity)

            def copy_wh(g, parity):
                c = Shape(HEADS[L])
                act.wait_ge(s["proj"], g + 1)
                src = ps[:, (2 + 2 * parity) * CH:(4 + 2 * parity) * CH].rearrange("p (q c) -> p q c", q=Q)
                nc.scalar.copy(wh_view(g * Q, Q, c)[:, :, :, 0:c.dh],
                               src[:, :, 0:D].rearrange("p q (h d) -> p q h d", h=c.H)).then_inc(s["proj_wh"], 1)

            for g in range(NC):
                group(g, g % 2)
            if L:
                copy_wh(NC - 1, 1)

        def load_function(L, i, function):
            at = 2 * (L - 1) + i
            nc.scalar.activation(warm[:, at:at + 1], ones_col[:, :], function)

        def layer_act(act, L):
            s, c = S[L], Shape(HEADS[L])
            H, w = c.H, c.w
            n = NT * H
            load_function(L, 0, ACT.Exp)
            h_relu(act, L)
            act.wait_ge(s["s_row_turned"], 1)
            nc.scalar.copy(s_row[0:n, :], ps[0:n, 6 * CH:6 * CH + P]).then_inc(s["s_row_copied"], 1)
            act.wait_ge(s["rel"], 1)
            nc.scalar.activation(ef[:, 0, 0:n], d_rel[:, 0:n], ACT.Exp).then_inc(s["ef"], 1)
            nc.scalar.activation(ef[:, 1, 0:n], d_rel[:, 0:n], ACT.Exp, scale=SLOPE).then_inc(s["ef"], 1)
            act.wait_ge(s["rel"], 3)
            nc.scalar.activation(ab[:, :, 0:n], s_lim[:, :, 0:n], ACT.Exp).then_inc(s["ef"], 1)
            load_function(L, 1, ACT.Sigmoid)

            def high(g):
                act.wait_ge(s["prod"], 2 * (g + 1))
                nc.scalar.copy(table_view(g, 0, c), prod_slot(g, c)).then_inc(s["hi"], 1)

            def middle(g, slot):
                act.wait_ge(s["r1"], g + 1)
                nc.scalar.copy(table_view(g, 1, c), prod_view(rest, slot, c)).then_inc(s["mid"], 1)

            for g in range(NC + 1):
                if g < NC:
                    high(g)
                if g > 0:
                    middle(g - 1, (g - 1) % RESTS)

            act.wait_ge(s["neg"], 3 if c.split else 2)

            def sweep(row, h, gi, sw, flip):
                for i, k in enumerate(ON_ACT):
                    if due(sw, 1) or i >= GATES:
                        act.wait_ge(s["gate_used"], gi + i + 1 - GATES)
                    at = h + k * H
                    nc.scalar.activation(gates[:, i % GATES, :], row, ACT.Sigmoid,
                                         bias=steep_d[:, 1 if flip else 0, at:at + 1],
                                         scale=-STEEP if flip else STEEP).then_inc(s["gate"], 1)

            def pair(m, parity):
                act.wait_ge(s["s_bc_in"], 16 * (m + 1))
                for hf in range(2):
                    sw = m * 2 + hf
                    sweep(s_row_of(c, parity, hf), head_of(c, parity, hf), held(act, sw * len(ON_ACT)), sw, c.split and hf)

            each_pair(act, c, pair)

        @block.scalar
        def _(act):
            for g in range(NC):
                act.wait_ge(ks_turned, g + 1)
                nc.scalar.copy(ks_T[:, g * CH:(g + 1) * CH], ps[:, (g % 2) * CH:(g % 2 + 1) * CH]).then_inc(ks_copied, 1)
            h_relu(act, 0)
            act.wait_ge(set_up, 11)

            def step(t, parity, scores=True, probs=True):
                v, vp = t - 1, 1 - parity
                for ch in range(NC):
                    if probs:
                        nv = v * NC + ch
                        if ch == 0:
                            act.wait_ge(neg_ready, v + 1)
                            if due(v, 1):
                                act.wait_ge(row_step, 3 * v - 2)
                        sl = score[:, vp, ch * CH:(ch + 1) * CH]
                        nc.scalar.activation(sl, sl, ACT.Exp, bias=neg_max[:, vp:vp + 1],
                                             accum_out=row_sum[:, vp, ch:ch + 1]).then_inc(p_ready, 1)
                    if scores:
                        n = t * NC + ch
                        act.wait_ge(s_ready, n + 1)
                        if due(n, 4):
                            act.wait_ge(score_ready, n - 3)
                        nc.scalar.activation(relu4[:, ch % 4, :], ps[:, (ch % 4) * CH:(ch % 4 + 1) * CH], ACT.Relu,
                                             scale=1.0 / SLOPE - 1.0).then_inc(relu_ready, 1)
                        act.wait_ge(mt_turned, n + 1)
                        if ch == 0 and due(t, 2):
                            act.wait_ge(adjT_stored[parity], 16 * (t // 2))
                        mt = ps_b[:, 4 * 2 * CH:4 * 2 * CH + CH]
                        nc.scalar.activation(adjT_out[:, parity, ch * Q:(ch + 1) * Q, :].rearrange("p t c -> p (t c)"),
                                             mt, ACT.Identity, bias=ones_col[:, 0:1]).then_inc(mt_copied, 1)

            step(0, 0, probs=False)
            step(1, 1)
            with act.Fori(1, NT // 2, 1) as t_at:
                t = t_at * 2
                step(t, 0)
                step(t + 1, 1)
            step(NT, 0, scores=False)

            for L in HEADS:
                layer_act(act, L)
            for g in range(NC):
                act.wait_ge(tail["neg"], g + 1)
                o = group_rows(o_all, g)
                nc.scalar.activation(o, o, ACT.Exp).then_inc(tail["exp"], 1)

        def tile_stats(dve, L, t, n):
            for k in range(n):
                nc.vector.bn_stats(stats[:, bass.ds(t + k, 1), :].rearrange("p a b -> p (a b)"),
                                   x_sb[:, bass.ds(t + k, 1), :].rearrange("p a b -> p (a b)")).then_inc(S[L]["stat"], 1)

        def layer_norm(dve, L):
            s = S[L]
            buf = norm0 if L == 0 else norm
            if L == 1:
                layer0_stored(dve)

            def group(g, parity):
                done = (g * Q) // STAT_TILES + 1 if L == 0 else (g + 1) * Q if L == 1 else g + 1
                dve.wait_ge(s["stat_step"], done * STATS)
                if due(g, 2):
                    dve.wait_ge(s["h_turned"], g - 1)
                for q in range(Q):
                    t = g * Q + q
                    nc.vector.tensor_scalar(buf[:, parity, q, :], x_sb[:, bass.ds(t, 1), :].rearrange("p a b -> p (a b)"),
                                            mean[:, bass.ds(t, 1)], rstd[:, bass.ds(t, 1)],
                                            ALU.subtract, ALU.mult).then_inc(s["normed"], 1)
                if L and due(g, 2):
                    after_projection(g - 2, parity)

            def after_projection(g, parity):
                c = Shape(HEADS[L])
                dve.wait_ge(s["proj_wh"], g + 1)
                src = ps[:, (2 + 2 * parity) * CH:(4 + 2 * parity) * CH].rearrange("p (q c) -> p q c", q=Q)
                nc.vector.tensor_copy(
                    sd[:, :, 0:NT * c.H].rearrange("p e (h t) -> p t e h", h=c.H)[:, bass.ds(g * Q, Q)],
                    src[:, :, D:D + 2 * c.H].rearrange("p t (e h) -> p t e h", e=2)).then_inc(s["proj_sd"], 1)

            for g in range(NC):
                group(g, g % 2)
                if L >= 2 and g == 3:
                    dve.wait_ge(x_ready[L - 1], X_DONE[L - 1])
                    tile_stats(dve, L, (NC - 1) * Q, Q)
            if L:
                after_projection(NC - 2, 0)
                after_projection(NC - 1, 1)

        def elu_parts(dve, g):
            o, xv = group_rows(o_all, g), group_rows(x_sb, g)
            nc.vector.scalar_tensor_tensor(out=xv, in0=o, scalar=0.0, in1=xv, op0=ALU.max, op1=ALU.add
                                           ).then_inc(tail["sum"], 1)
            nc.vector.tensor_scalar(o, o, 0.0, None, ALU.min).then_inc(tail["neg"], 1)

        def elu_sum(dve, g):
            dve.wait_ge(tail["exp"], g + 1)
            dve.wait_ge(tail["sum"], g + 1)
            xv = group_rows(x_sb, g)
            nc.vector.scalar_tensor_tensor(out=xv, in0=group_rows(o_all, g), scalar=-1.0, in1=xv,
                                           op0=ALU.add, op1=ALU.add).then_inc(tail["y"], 1)

        def layer_dve(dve, L):
            s, c = S[L], Shape(HEADS[L])
            H, dh, w = c.H, c.dh, c.w
            n = NT * H
            dve.wait_ge(s["proj_sd"], NC)
            nc.vector.tensor_reduce(d_max[:, 0:H], sd[:, 1, 0:n].rearrange("p (h t) -> p h t", h=H), AX_X, ALU.max
                                    ).then_inc(s["d_max"], 1)
            flat = lambda a: a.rearrange("p (t h) -> p t h", h=H)
            sv, dv = (sd[:, e, 0:n].rearrange("p (h t) -> p t h", h=H) for e in range(2))
            nc.vector.tensor_scalar(flat(neg_d[:, 0:n]), dv, -1.0, None, ALU.mult).then_inc(s["neg"], 1)
            nc.vector.tensor_scalar(flat(steep_d[:, 0, 0:n]), dv, STEEP, None, ALU.mult).then_inc(s["neg"], 1)
            if c.split:
                nc.vector.tensor_scalar(flat(steep_d[:, 1, 0:n]), dv, -STEEP, None, ALU.mult).then_inc(s["neg"], 1)
            dve.wait_ge(s["d_top"], 1)
            tb = d_top[:, 0:H].unsqueeze(1).to_broadcast([P, NT, H])
            nc.vector.tensor_tensor(flat(d_rel[:, 0:n]), dv, tb, ALU.subtract).then_inc(s["rel"], 1)
            nc.vector.tensor_tensor(flat(s_top[:, 0:n]), sv, tb, ALU.add).then_inc(s["s_top"], 1)
            dve.wait_ge(s["s_top"], 1)
            nc.vector.tensor_scalar(s_lim[:, 0, 0:n], s_top[:, 0:n], 1.0 - SLOPE, 0.0, ALU.mult, ALU.min).then_inc(s["rel"], 1)
            nc.vector.tensor_scalar(s_lim[:, 1, 0:n], s_top[:, 0:n], SLOPE - 1.0, 0.0, ALU.mult, ALU.min).then_inc(s["rel"], 1)

            def product(g):
                pv = prod_slot(g, c).rearrange("p t (h e) w -> p t h e w", e=2)
                efv = ef[:, :, 0:n].rearrange("p e (t h) -> p e t h", h=H)
                if g >= PRODS:
                    dve.wait_ge(s["hi"], g - PRODS + 1)
                    dve.wait_ge(s["r1"], g - PRODS + 1)
                for e in range(2):
                    nc.vector.tensor_tensor(
                        pv[:, :, :, e, :], wh_view(g * Q, Q, c),
                        efv[:, e, bass.ds(g * Q, Q), :].unsqueeze(3).to_broadcast([P, Q, H, w]), ALU.mult).then_inc(s["prod"], 1)

            def first_rest(g, slot):
                dve.wait_ge(s["hi"], g + 1)
                if g >= RESTS:
                    dve.wait_ge(s["table"], g - RESTS + 1)
                nc.vector.tensor_tensor(prod_view(rest, slot, c), prod_slot(g, c), table_view(g, 0, c),
                                        ALU.subtract).then_inc(s["r1"], 1)

            dve.wait_ge(s["ef"], 3)
            dve.wait_ge(s["proj_wh"], NC)
            dve.wait_ge(s["ones"], 1)
            for g in range(NC + 1):
                if g < NC:
                    product(g)
                if g > 0:
                    first_rest(g - 1, (g - 1) % RESTS)

            dve.wait_ge(s["neg"], 3 if c.split else 2)

            def sweep(row, h, gi, u, sw, mask_at, flip, between, later):
                for k in range(NT):
                    slot = k % RING
                    if k == REDUCE_AT:
                        between()
                    if k == STATS_AT:
                        later()
                    if k % 2 == 0 and (due(sw, 1) or k >= RING):
                        dve.wait_ge(s["step_used"], u + (k + 2 - RING))
                    dst = steps[:, slot, :].rearrange("p (q c) -> p q c", q=Q)
                    mk = run(adjT_b, mask_at + k * P * 2, P, BF16)
                    if k in ON_ACT:
                        i = ON_ACT.index(k)
                        dve.wait_ge(s["gate"], gi + i + 1)
                        nc.vector.tensor_tensor(dst, gates[:, i % GATES, :].rearrange("p (q c) -> p q c", q=Q), mk, ALU.mult
                                                ).then_inc(s["gate_used"], 1)
                    else:
                        at = h + k * H
                        nc.vector.scalar_tensor_tensor(out=dst, in0=row, scalar=neg_d[:, at:at + 1], in1=mk,
                                                       op0=ALU.is_lt if flip else ALU.is_ge, op1=ALU.mult
                                                       ).then_inc(s["step"], 1)

            def reduce(m, parity, hf):
                sw = m * 2 + hf
                dve.wait_ge(s["step_used"], (sw + 1) * NT)
                if due(m, 1):
                    dve.wait_ge(x_ready[L], m)
                if c.split:
                    src = ps[:, hf * 4 * CH:(hf + 1) * 4 * CH].rearrange("p (q c) -> p q c", q=Q)[:, :, 0:3 * w]
                    nc.vector.tensor_reduce(red[:, hf, 0:Q * w].rearrange("p (q w) -> p q w", q=Q),
                                            src.rearrange("p q (s w) -> p q w s", s=3), AX_X, ALU.add).then_inc(s["reduced"], 1)
                    return
                if hf:
                    a0 = (4 + 2 * parity) * CH
                    srca = ps[:, a0:a0 + 2 * CH].rearrange("p (q c) -> p q c", q=Q)[:, :, 0:6 * w]
                    nc.vector.tensor_reduce(red_a[:, 0:Q * 2 * w].rearrange("p (q h w) -> p q h w", q=Q, h=2),
                                            srca.rearrange("p q (h s w) -> p q h w s", h=2, s=3), AX_X, ALU.add)
                src = ps[:, 2 * hf * CH:(2 * hf + 2) * CH].rearrange("p (q c) -> p q c", q=Q)[:, :, 0:6 * w]
                nc.vector.tensor_reduce(red[:, hf, 0:Q * 2 * w].rearrange("p (q e w) -> p q e w", q=Q, e=2),
                                        src.rearrange("p q (e s w) -> p q e w s", e=2, s=3), AX_X, ALU.add).then_inc(s["reduced"], 1)

            def pair(m, parity):
                dve.wait_ge(s["s_bc_in"], 16 * (m + 1))
                dve.wait_ge(s["adjT_in"], 16 * (ig_of(L, m) + 1))
                for hf in range(2):
                    sw = m * 2 + hf
                    if hf:
                        between = lambda: reduce(m, parity, 0)
                    else:
                        between = (lambda: reduce(m - 1, 1 - parity, 1)) if due(m, 1) else (lambda: None)
                    if hf == 0 and due(m, 1) and (c.split or parity == 0):
                        later = lambda: after_group(m)
                    else:
                        later = lambda: None
                    sweep(s_row_of(c, parity, hf).rearrange("p (q c) -> p q c", q=Q), head_of(c, parity, hf),
                          held(dve, sw * len(ON_ACT)), held(dve, sw * NT), sw,
                          held(dve, adjT_half(c, m, parity, hf)), c.split and hf, between, later)

            def after_group(m):
                dve.wait_ge(x_ready[L], m)
                g = ig_of(L, m) - 1
                if L < 3:
                    tile_stats(dve, L + 1, g * Q, Q)
                else:
                    elu_parts(dve, g)

            each_pair(dve, c, pair)
            reduce(NC * c.pairs - 1, 1, 1)

        @block.vector
        def _(dve):
            for i in range(PIECES):
                dve.wait_ge(x_loaded[i], 16)
                tile_stats(dve, 0, i * NT // PIECES, NT // PIECES)
            layer_norm(dve, 0)
            dve.wait_ge(w_turned, 1)
            nc.vector.tensor_copy(w_turn[:, :, :].rearrange("p a b -> p (a b)"), ps[:, 6 * CH:6 * CH + 3 * P]).then_inc(w_copied, 1)
            dve.wait_ge(wa_ready, 1)
            for i, L in enumerate(HEADS):
                w = w_turn[:, 0, :] if i == 0 else w_in[:, i, :]
                nc.vector.tensor_copy(w_ext[L][:, 0:D], w).then_inc(w_done, 1)
                nc.vector.tensor_copy(w_ext[L][:, D:D + 2 * HEADS[L]],
                                      ps[:, 7 * CH + 8 * i:7 * CH + 8 * i + 2 * HEADS[L]]).then_inc(w_done, 1)

            def cast(t, parity, ch):
                nc.vector.tensor_scalar(mask[:, parity, ch * CH:(ch + 1) * CH], adj_in[:, parity, ch * CH:(ch + 1) * CH],
                                        0.0, -1.0, ALU.is_gt, ALU.add).then_inc(mask_ready, 1)

            def update(v, parity, last=False):
                dve.wait_ge(p_ready, (v + 1) * NC)
                nc.vector.tensor_reduce(den0[:, parity:parity + 1], row_sum[:, parity, :], AX_X, ALU.add).then_inc(row_step, 1)
                done = 3 * v + 2 - last
                dve.wait_ge(row_step, done + 1)
                nc.vector.reciprocal(rden0[:, parity:parity + 1], den0[:, parity:parity + 1]).then_inc(row_step, 1)
                dve.wait_ge(row_step, done + 2)
                dve.wait_ge(prob_used, (v + 1) * NC)
                xv = x_sb[:, bass.ds(v, 1), :].rearrange("p a d -> p (a d)")
                nc.vector.scalar_tensor_tensor(out=xv, in0=ps[:, 7 * CH:7 * CH + D],
                                               scalar=rden0[:, parity:parity + 1], in1=xv,
                                               op0=ALU.mult, op1=ALU.add).then_inc(x_ready[0], 1)

            def step(t, parity):
                scores, nxt = live(t), live(t + 1)
                for ch in range(NC if live(t - 1) or scores else LAG):
                    if ch == LAG + 1 and live(t - 2):
                        update(t - 2, parity)
                    if nxt and ch == 0:
                        dve.wait_ge(adj_loaded[1 - parity], 16 * ((t + 1) // 2 + 1))
                    if nxt and due(t, 1):
                        dve.wait_ge(mt_turned, (t - 1) * NC + ch + 1)
                    if scores:
                        if due(t, 2) and ch == 0:
                            dve.wait_ge(turned, (t - 1) * NC - LAG)
                        if due(t, 2) and ch == NC - LAG:
                            dve.wait_ge(turned, (t - 1) * NC)
                        dve.wait_ge(relu_ready, t * NC + ch + 1)
                    if nxt:
                        cast(t + 1, 1 - parity, ch)
                    if scores:
                        nc.vector.tensor_tensor_reduce(
                            out=score[:, parity, ch * CH:(ch + 1) * CH], in0=ps[:, (ch % 4) * CH:(ch % 4 + 1) * CH],
                            in1=relu4[:, ch % 4, :], scale=SLOPE, scalar=-3e38, op0=ALU.add, op1=ALU.max,
                            accum_out=row_max[:, parity, ch:ch + 1]).then_inc(score_ready, 1)
                    v, cc = lagging(t, ch, LAG)
                    if live(v):
                        nv = v * NC + cc
                        dve.wait_ge(turned, nv + 1)
                        if due(nv, 4):
                            dve.wait_ge(prob_used, nv - 3)
                        nc.vector.tensor_copy(prob_T[:, cc % 4, :], ps[:, (5 + cc % 2) * CH:(6 + cc % 2) * CH]).then_inc(prob_ready, 1)
                    if ch == LAG + 3 and live(t - 2):
                        dve.wait_ge(x_ready[0], t - 1)
                        tile_stats(dve, 1, t - 2, 1)
                if scores:
                    dve.wait_ge(score_ready, (t + 1) * NC)
                    if due(t, 2):
                        dve.wait_ge(p_ready, (t - 1) * NC)
                    nc.vector.tensor_reduce(row_top[:, parity:parity + 1], row_max[:, parity, :], AX_X, ALU.max).then_inc(row_step, 1)
                    dve.wait_ge(row_step, top_count(t))
                    nc.vector.tensor_scalar(neg_max[:, parity:parity + 1], row_top[:, parity:parity + 1], -1.0, None,
                                            ALU.mult).then_inc(neg_ready, 1)

            def top_count(t):
                return t + 1 if isinstance(t, int) and t < 2 else 3 * t - 1

            dve.wait_ge(adj_loaded[0], 16)
            for ch in range(NC):
                cast(0, 0, ch)
            step(0, 0)
            step(1, 1)
            with dve.Fori(1, NT // 2 - 1, 1) as t_at:
                t = t_at * 2
                step(t, 0)
                step(t + 1, 1)
            for t in range(NT - 2, NT + 2):
                step(t, t % 2)
            update(NT - 1, 1, last=True)
            dve.wait_ge(x_ready[0], NT)
            tile_stats(dve, 1, NT - 1, 1)

            for L in HEADS:
                layer_norm(dve, L)
                layer_dve(dve, L)
            for g in range(NC - 1):
                elu_sum(dve, g)
            dve.wait_ge(x_ready[3], X_DONE[3])
            elu_parts(dve, NC - 1)
            elu_sum(dve, NC - 1)

        def h_turn(pe, L):
            s = S[L]
            buf = norm0 if L == 0 else norm

            def group(g, parity):
                pe.wait_ge(s["normed"], (g + 1) * Q)
                if due(g, 2):
                    pe.wait_ge(s["h_done"], g - 1)
                for q in range(Q):
                    last = nc.tensor.transpose(ps[:, parity * CH + q * P:parity * CH + (q + 1) * P],
                                               buf[:, parity, q, :], ident[:, :])
                last.then_inc(s["h_turned"], 1)
                if L and due(g, 1):
                    project(g - 1, 1 - parity)

            def project(g, parity):
                c = Shape(HEADS[L])
                pe.wait_ge(s["h_done"], g + 1)
                if due(g, 2):
                    pe.wait_ge(s["proj_wh"], g - 1)
                    pe.wait_ge(s["proj_sd"], g - 1)
                for q in range(Q):
                    at = (2 + 2 * parity) * CH + q * 2 * P
                    last = nc.tensor.matmul(ps[:, at:at + D + 2 * c.H], h_grp[:, parity, q * P:(q + 1) * P],
                                            w_ext[L][:, :], start=True, stop=True, skip_group_check=True)
                last.then_inc(s["proj"], 1)

            for g in range(NC):
                group(g, g % 2)
            if L:
                project(NC - 1, 1)
                n = NT * HEADS[L]
                pe.wait_ge(s["proj_sd"], NC)
                nc.tensor.transpose(ps[0:n, 6 * CH:6 * CH + P], sd[:, 0, 0:n],
                                    ident[:, :]).then_inc(s["s_row_turned"], 1)

        def layer_pe(pe, L):
            s, c = S[L], Shape(HEADS[L])
            w = c.w
            pe.wait_ge(s["proj_sd"], NC)

            def sweep(head, gi, ni, mask_at, parity, hf, start_up):
                for k in range(NT):
                    slot = k % RING
                    if k in ON_ACT:
                        pe.wait_ge(s["gate_used"], gi + ON_ACT.index(k) + 1)
                    else:
                        pe.wait_ge(s["step"], ni + ALONE.index(k) + 1)
                    if start_up and k % Q == 0:
                        pe.wait_ge(s["table"], k // Q + 1)
                    start = k == 0
                    tab = k * TROW + head * 6 * w
                    if c.split:
                        rows = table[:, tab + hf * 3 * w:tab + (hf + 1) * 3 * w]
                        for q in range(Q):
                            at = (hf * 4 + q) * CH
                            last = nc.tensor.matmul(ps[:, at:at + 3 * w], steps[:, slot, q * P:(q + 1) * P], rows,
                                                    start=start, stop=False, skip_group_check=True)
                    else:
                        rows = table[:, tab:tab + 6 * w]
                        by_mask = k % 2 == hf
                        both = table[:, tab - hf * 6 * w:tab + (2 - hf) * 6 * w].rearrange("p (h e c) -> p h e c", h=2, e=2)
                        for q in range(Q):
                            at = 2 * hf * CH + q * 2 * P
                            last = nc.tensor.matmul(ps[:, at:at + 6 * w], steps[:, slot, q * P:(q + 1) * P], rows,
                                                    start=start and q % 2 == 0, stop=False, skip_group_check=True)
                            if by_mask:
                                at = (4 + 2 * parity) * CH + q * 2 * P
                                mk = run(adjT_b[:, q], mask_at + k * P * 2, P, BF16)
                                last = nc.tensor.matmul(ps[:, at:at + 6 * w], mk, both[:, :, 1, :],
                                                        start=start and q % 2 == 0, stop=False, skip_group_check=True)
                    last.then_inc(s["step_used"], 1)

            def pair(m, parity):
                pe.wait_ge(s["adjT_in"], 16 * (ig_of(L, m) + 1))
                for hf in range(2):
                    sw = m * 2 + hf
                    if due(sw, 2):
                        pe.wait_ge(s["reduced"], sw - 1)
                    sweep(head_of(c, parity, hf), held(pe, sw * len(ON_ACT)), held(pe, sw * len(ALONE)),
                          held(pe, adjT_half(c, m, parity, hf)), parity, hf, not due(sw, 2 if c.split else 1))

            each_pair(pe, c, pair)

        @block.tensor
        def _(pe):
            pe.wait_ge(set_up, 11)
            for g in range(NC):
                if g % (NC // PIECES) == 0:
                    pe.wait_ge(ks_loaded[g // (NC // PIECES)], 16)
                if g >= 2:
                    pe.wait_ge(ks_copied, g - 1)
                for q in range(Q):
                    last = nc.tensor.transpose(ps[:, (g % 2) * CH + q * P:(g % 2) * CH + (q + 1) * P],
                                               ks_nat[:, g * Q + q, :], ident[:, :])
                last.then_inc(ks_turned, 1)
            pe.wait_ge(ks_copied, NC)
            h_turn(pe, 0)
            pe.wait_ge(loaded["w"], 48)
            for i in range(3):
                last = nc.tensor.transpose(ps[:, 6 * CH + i * P:6 * CH + (i + 1) * P], w_in[:, i, :], ident[:, :])
            last.then_inc(w_turned, 1)
            pe.wait_ge(w_copied, 1)
            pe.wait_ge(loaded["a"], 16 * A_LOADS)
            for i in range(3):
                w = w_in[:, 0, :] if i == 0 else w_turn[:, i, :]
                last = nc.tensor.matmul(ps[:, 7 * CH + 8 * i:7 * CH + 8 * i + 8], w, a_blk[:, i, :], start=True, stop=True,
                                        skip_group_check=True)
            last.then_inc(wa_ready, 1)
            pe.wait_ge(S[0]["h_done"], NC)
            pe.wait_ge(w_done, 6)

            def step(t, parity):
                for ch in range(NC if live(t - 1) or live(t) else LAG + 1):
                    if live(t):
                        n = t * NC + ch
                        if ch == 0:
                            pe.wait_ge(h_tile_ready, t + 1)
                        if due(n, 4):
                            pe.wait_ge(score_ready, n - 3)
                        pe.wait_ge(mask_ready, n + 1)
                        bank = ps[:, (ch % 4) * CH:(ch % 4 + 1) * CH]
                        nc.tensor.matmul(bank, h_tile[:, parity, :], ks_T[:, ch * CH:(ch + 1) * CH], start=True, stop=False)
                        nc.tensor.matmul(bank, big_ident[:, :], mask[:, parity, ch * CH:(ch + 1) * CH],
                                         start=False, stop=True).then_inc(s_ready, 1)
                        if due(n, 1):
                            pe.wait_ge(mt_copied, n)
                        for q in range(Q):
                            at = 4 * 2 * CH + q * P
                            last = nc.tensor.transpose(ps_b[:, at:at + P],
                                                       mask[:, parity, ch * CH + q * P:ch * CH + (q + 1) * P], identb[:, :])
                        last.then_inc(mt_turned, 1)
                    v, cc = lagging(t, ch, LAG)
                    if live(v):
                        nv, vp = v * NC + cc, (parity + (ch >= LAG)) % 2
                        pe.wait_ge(p_ready, nv + 1)
                        if due(nv, 2):
                            pe.wait_ge(prob_ready, nv - 1)
                        for q in range(Q):
                            at = (5 + cc % 2) * CH + q * P
                            last = nc.tensor.transpose(ps[:, at:at + P],
                                                       score[:, vp, cc * CH + q * P:cc * CH + (q + 1) * P], ident[:, :])
                        last.then_inc(turned, 1)
                    v, cc = lagging(t, ch, LAG + 1)
                    if live(v):
                        nv = v * NC + cc
                        pe.wait_ge(prob_ready, nv + 1)
                        if cc == 0 and due(v, 1):
                            pe.wait_ge(x_ready[0], v)
                        for q in range(Q):
                            last = nc.tensor.matmul(ps[:, 7 * CH:7 * CH + D],
                                                    prob_T[:, cc % 4, q * P:(q + 1) * P], ks_nat[:, cc * Q + q, :],
                                                    start=(cc == 0 and q == 0), stop=(cc == NC - 1 and q == Q - 1),
                                                    skip_group_check=True)
                        last.then_inc(prob_used, 1)

            step(0, 0)
            step(1, 1)
            with pe.Fori(1, NT // 2, 1) as t_at:
                t = t_at * 2
                step(t, 0)
                step(t + 1, 1)
            step(NT, 0)
            step(NT + 1, 1)

            for L in HEADS:
                h_turn(pe, L)
                layer_pe(pe, L)


_INS = ["x", "adj", "L0_gnn_ks", "L1_gnn_W", "L1_gnn_attn_src", "L1_gnn_attn_dst", "L2_gnn_W", "L2_gnn_a",
        "L3_gnn_W", "L3_gnn_a"]


def kernel(**inputs):
    import numpy as _np
    import concourse.bacc as _bacc
    from concourse import mybir as _mybir
    from concourse.bass_utils import run_bass_kernel_spmd as _run

    nc = _bacc.Bacc("TRN2", target_bir_lowering=False, num_devices=1)
    arrays, args = {}, []
    for name in _INS:
        a = _np.ascontiguousarray(inputs[name])
        arrays[f"in_{name}_dram"] = a
        args.append(nc.dram_tensor(f"in_{name}_dram", a.shape, _mybir.dt.from_np(a.dtype), kind="ExternalInput").ap())
    args.append(nc.dram_tensor("out_0_dram", (N, D), F32, kind="ExternalOutput").ap())
    bass_gnn_stack_kernel(nc, *args)
    r = _run(nc, [arrays], core_ids=[0])
    return r.results[0]["out_0_dram"]
```
